# Optimizing a Trainium2 kernel written in Bass

```python
import numpy as np
import jax
import jax.numpy as jnp

def _softmax(x, axis=-1):
    return jax.nn.softmax(x, axis=axis)

def _gelu(x):
    return jax.nn.gelu(x, approximate=True)

def _silu(x):
    return jax.nn.silu(x)

def _sigmoid(x):
    return jax.nn.sigmoid(x)

def _layernorm(x, axis=-1, eps=1e-05):
    m = jnp.mean(x, axis=axis, keepdims=True)
    v = jnp.var(x, axis=axis, keepdims=True)
    return (x - m) / jnp.sqrt(v + eps)

def _scatter_add(tgt, idx, src, axis=0):
    return tgt.at[idx].add(src)

def _segment_sum(src, seg, n):
    return jax.ops.segment_sum(src, seg, n)
kernel_name = 'mk_adj_seq_d2_adj_r2_1f9991'

def setup_inputs(seed: int=0):
    np.random.seed(seed)
    _w = jnp.asarray

    def _rec_inputs():
        import jax
        import jax.numpy as jnp
        _gk = jax.random.key(seed)
        x = 7.22e-05 + 1 * jax.random.normal(jax.random.fold_in(_gk, 1), (16, 512, 256), jnp.float32)
        _a = jax.random.bernoulli(jax.random.fold_in(_gk, 2), 0.0078125, (16, 512, 512))
        _a = jnp.logical_or(_a, jnp.swapaxes(_a, -1, -2))
        _a = jnp.logical_or(_a, jnp.eye(512, dtype=bool))
        adj = _a.astype(jnp.int32)
        return (x, adj)
    x, adj = _rec_inputs()

    def _L0_gnn_setup():
        import jax, jax.numpy as jnp
        import numpy as np
        B, N, E, FF, L = (8, 1024, 256, 128, 2)
        LN_EPS = 1e-05
        SCALE = float(np.sqrt(FF))

        def layer_norm(x, g, b):
            m = jnp.mean(x, axis=-1, keepdims=True)
            v = jnp.mean(jnp.square(x - m), axis=-1, keepdims=True)
            return (x - m) * jax.lax.rsqrt(v + LN_EPS) * g + b
        key = jax.random.key(seed)
        ks = jax.random.split(key, 9)
        s = 0.02
        node_fts = jax.random.normal(ks[0], (B, N, E), jnp.float32)
        rel_edges = jax.random.randint(ks[1], (B, N, N), 0, 2, jnp.int32)
        Wq = jax.random.normal(ks[2], (L, FF, E), jnp.float32) * s
        bq = jnp.zeros((L, FF), jnp.float32)
        Wk = jax.random.normal(ks[3], (L, FF, E), jnp.float32) * s
        bk = jnp.zeros((L, FF), jnp.float32)
        Wc = jax.random.normal(ks[4], (L, E, E), jnp.float32) * s
        ln_g = jnp.ones((L, E), jnp.float32)
        ln_b = jnp.zeros((L, E), jnp.float32)
        return {'node_fts': node_fts, 'rel_edges': rel_edges, 'Wq': Wq, 'bq': bq, 'Wk': Wk, 'bk': bk, 'Wc': Wc, 'ln_g': ln_g, 'ln_b': ln_b}
    _L0_gnn_all = _L0_gnn_setup()
    _L0_gnn_in = {k: v for k, v in _L0_gnn_all.items() if k in ('Wq', 'bq', 'Wk', 'bk', 'Wc', 'ln_g', 'ln_b')}
    del _L0_gnn_all

    def _L1_gnn_setup():
        import jax, jax.numpy as jnp
        import numpy as np
        B, N, D, H = (4, 1024, 256, 8)
        HD = D // H
        EPS = 1e-05
        key = jax.random.key(seed)
        ks = jax.random.split(key, 12)
        x = jax.random.normal(ks[0], (B, N, D), dtype=jnp.float32)
        adj = jax.random.randint(ks[1], (B, N, N), 0, 2, dtype=jnp.int32)
        adj = jnp.maximum(adj, jnp.eye(N, dtype=jnp.int32)[None, :, :])
        s = 1.0 / np.sqrt(D)
        Wq = jax.random.uniform(ks[2], (D, D), jnp.float32, -s, s)
        bq = jnp.zeros((D,), jnp.float32)
        Wk = jax.random.uniform(ks[3], (D, D), jnp.float32, -s, s)
        bk = jnp.zeros((D,), jnp.float32)
        Wv = jax.random.uniform(ks[4], (D, D), jnp.float32, -s, s)
        bv = jnp.zeros((D,), jnp.float32)
        Wo = jax.random.uniform(ks[5], (D, D), jnp.float32, -s, s)
        bo = jnp.zeros((D,), jnp.float32)
        gamma = jnp.ones((D,), jnp.float32)
        beta = jnp.zeros((D,), jnp.float32)
        return {'x': x, 'adj': adj, 'Wq': Wq, 'bq': bq, 'Wk': Wk, 'bk': bk, 'Wv': Wv, 'bv': bv, 'Wo': Wo, 'bo': bo, 'gamma': gamma, 'beta': beta}
    _L1_gnn_all = _L1_gnn_setup()
    _L1_gnn_in = {k: v for k, v in _L1_gnn_all.items() if k in ('Wq', 'bq', 'Wk', 'bk', 'Wv', 'bv', 'Wo', 'bo', 'gamma', 'beta')}
    del _L1_gnn_all
    return {'x': x, 'adj': adj, 'L0_gnn_Wq': _L0_gnn_in['Wq'], 'L0_gnn_bq': _L0_gnn_in['bq'], 'L0_gnn_Wk': _L0_gnn_in['Wk'], 'L0_gnn_bk': _L0_gnn_in['bk'], 'L0_gnn_Wc': _L0_gnn_in['Wc'], 'L0_gnn_ln_g': _L0_gnn_in['ln_g'], 'L0_gnn_ln_b': _L0_gnn_in['ln_b'], 'L1_gnn_Wq': _L1_gnn_in['Wq'], 'L1_gnn_bq': _L1_gnn_in['bq'], 'L1_gnn_Wk': _L1_gnn_in['Wk'], 'L1_gnn_bk': _L1_gnn_in['bk'], 'L1_gnn_Wv': _L1_gnn_in['Wv'], 'L1_gnn_bv': _L1_gnn_in['bv'], 'L1_gnn_Wo': _L1_gnn_in['Wo'], 'L1_gnn_bo': _L1_gnn_in['bo'], 'L1_gnn_gamma': _L1_gnn_in['gamma'], 'L1_gnn_beta': _L1_gnn_in['beta']}

def reference(x, adj, L0_gnn_Wq, L0_gnn_bq, L0_gnn_Wk, L0_gnn_bk, L0_gnn_Wc, L0_gnn_ln_g, L0_gnn_ln_b, L1_gnn_Wq, L1_gnn_bq, L1_gnn_Wk, L1_gnn_bk, L1_gnn_Wv, L1_gnn_bv, L1_gnn_Wo, L1_gnn_bo, L1_gnn_gamma, L1_gnn_beta):
    import jax
    import jax.numpy as jnp

    def _L0_gnn_ref(node_fts, rel_edges, Wq, bq, Wk, bk, Wc, ln_g, ln_b):
        import jax, jax.numpy as jnp
        import numpy as np
        B, N, E, FF, L = (8, 1024, 256, 128, 2)
        LN_EPS = 1e-05
        SCALE = float(np.sqrt(FF))

        def layer_norm(x, g, b):
            m = jnp.mean(x, axis=-1, keepdims=True)
            v = jnp.mean(jnp.square(x - m), axis=-1, keepdims=True)
            return (x - m) * jax.lax.rsqrt(v + LN_EPS) * g + b
        x = node_fts
        mask = rel_edges == 0
        for k in range(L):
            q = jnp.einsum('bnd,fd->bnf', x, Wq[k]) + bq[k]
            kk = jnp.einsum('bnd,fd->bnf', x, Wk[k]) + bk[k]
            scores = jnp.einsum('bof,bif->boi', q, kk) / SCALE
            scores = jnp.where(mask, -10000000000.0, scores)
            attn = jax.nn.softmax(scores, axis=2)
            attn = jnp.where(mask, 0.0, attn)
            ctx = jnp.einsum('boi,bid->bod', attn, x)
            ctx = jnp.einsum('bnd,ed->bne', ctx, Wc[k])
            x = layer_norm(x + ctx, ln_g[k], ln_b[k])
        return x

    def _L1_gnn_ref(x, adj, Wq, bq, Wk, bk, Wv, bv, Wo, bo, gamma, beta):
        import jax, jax.numpy as jnp
        import numpy as np
        B, N, D, H = (4, 1024, 256, 8)
        HD = D // H
        EPS = 1e-05
        b, n, d = x.shape
        scale = 1.0 / np.sqrt(HD).astype(np.float32)
        q = (x @ Wq + bq).reshape(b, n, H, HD)
        k = (x @ Wk + bk).reshape(b, n, H, HD)
        v = (x @ Wv + bv).reshape(b, n, H, HD)
        scores = jnp.einsum('bnhd,bmhd->bhnm', q, k) * scale
        mask = (adj == 0)[:, None, :, :]
        scores = jnp.where(mask, jnp.float32(-jnp.inf), scores)
        attn = jax.nn.softmax(scores, axis=-1)
        h = jnp.einsum('bhnm,bmhd->bnhd', attn, v).reshape(b, n, d)
        h = h @ Wo + bo
        y = h + x
        mu = jnp.mean(y, axis=-1, keepdims=True)
        var = jnp.mean(jnp.square(y - mu), axis=-1, keepdims=True)
        return (y - mu) * jax.lax.rsqrt(var + EPS) * gamma + beta
    x = _L0_gnn_ref(x, adj, L0_gnn_Wq, L0_gnn_bq, L0_gnn_Wk, L0_gnn_bk, L0_gnn_Wc, L0_gnn_ln_g, L0_gnn_ln_b)
    x = _L1_gnn_ref(x, adj, L1_gnn_Wq, L1_gnn_bq, L1_gnn_Wk, L1_gnn_bk, L1_gnn_Wv, L1_gnn_bv, L1_gnn_Wo, L1_gnn_bo, L1_gnn_gamma, L1_gnn_beta)
    return x

_drawn_inputs = setup_inputs


def setup_inputs(seed=0):
    import zlib

    import numpy as np

    out = dict(_drawn_inputs(seed))
    spreads = {'L0_gnn_bq': (0.0, 0.8),
     'L0_gnn_bk': (0.0, 0.8),
     'L0_gnn_ln_g': (1.0, 0.2),
     'L0_gnn_ln_b': (0.0, 0.1),
     'L1_gnn_bq': (0.0, 0.8),
     'L1_gnn_bk': (0.0, 0.8),
     'L1_gnn_bv': (0.0, 0.1),
     'L1_gnn_bo': (0.0, 0.1),
     'L1_gnn_gamma': (1.0, 0.2),
     'L1_gnn_beta': (0.0, 0.1)}
    factors = {'L0_gnn_Wq': 3.66, 'L0_gnn_Wk': 3.491}
    for name, (base, spread) in spreads.items():
        noise = np.random.default_rng([zlib.crc32(name.encode()), seed]).standard_normal(out[name].shape)
        drawn = base * np.exp(spread * noise) if base else spread * noise
        out[name] = jnp.asarray(drawn.astype(out[name].dtype))
    for name, factor in factors.items():
        out[name] = (out[name] * factor).astype(out[name].dtype)
    return out
```

```python
from contextlib import ExitStack

import concourse.bass as bass
from concourse import mybir

P = 128
NB, N, D = 16, 512, 256
F = 128
H, HD = 8, 32
NT = N // P
DC = D // P
LN_EPS = 1e-5
L0_SCALE = float(F) ** -0.5
L1_SCALE = float(HD) ** -0.5
MASKED = -1e30
ALL_MASKED = 1e28
BIG = 3e38

LOOP_SLOTS = ([("H", h, "i") for h in range(4)] + [("L", 1, "i+1")]
              + [("H", h, "i") for h in range(4, 8)] + [("L", 0, "i+2")])
TAIL_SLOTS = [("H", h) for h in range(8)]
AHEAD = 3
PRO_SLOTS = 3
LOOPS = NB - 1

LOOP_JOBS = [
    ("AV", 0, "i+1", 0, (0, 1)), ("WC", 1, "i+1", 0, (2, 3)), ("V", 0, "i", 0, (5, 6)),
    ("X", 1, "i+1", 1, (9, 9)), ("QK", 0, "i+1", 1, (11, 11)),
    ("R", None, "i", 0, (15,)), ("OG", 1, "i", 0, (17, 18)),
    ("AV", 0, "i+1", 1, (20, 20)), ("WC", 1, "i+1", 1, (21, 22)),
    ("X", 0, "i+2", 0, (24, 24)), ("QK", 1, "i+2", 0, (26, 26)),
    ("X2", 0, "i+1", 0, (28, 28)), ("Q", 1, "i+1", 0, (30, 30)), ("K", 0, "i+1", 0, (31, 31)),
    ("R", None, "i", 1, (35,)), ("OG", 1, "i", 1, (37, 37)), ("WO", 0, "i", 0, (39, 39)),
]
PRO_JOBS = [
    [("X", 0, 0, 0), ("QK", 1, 0, 0)],
    [("AV", 0, 0, 0), ("WC", 1, 0, 0), ("X", 0, 0, 1), ("QK", 1, 0, 1)],
    [("X", 0, 1, 0), ("AV", 1, 0, 1), ("WC", 0, 0, 1), ("QK", 1, 1, 0), ("X2", 0, 0, 0), ("Q", 1, 0, 0), ("K", 0, 0, 0)],
]
TAIL_JOBS = [
    ("V", 0, 0, (2, 3)), ("R", None, 0, (14,)), ("OG", 1, 0, (15, 16)),
    ("R", None, 1, (30,)), ("OG", 1, 1, (31, 31)), ("WO", 0, 0, (31, 31)),
]
DVE_TILE = 3
LAST_ACT_TILE = 2


def graph_attention(nc, x, adj, l0, l1, out):
    fp32, fp16, bf16, i32 = mybir.dt.float32, mybir.dt.float16, mybir.dt.bfloat16, mybir.dt.int32
    ALU, ACT = mybir.AluOpType, mybir.ActivationFunctionType

    x_v = x.rearrange("b (t p) d -> b p t d", p=P)
    adj_v = adj.rearrange("b (t p) k -> b p t k", p=P)
    out_v = out.rearrange("b (t p) d -> b p t d", p=P)

    ctx = ExitStack()
    with ctx:
        def sb(name, shape, dt=fp32):
            return ctx.enter_context(nc.sbuf_tensor(name, shape, dt))

        def sem(name):
            return ctx.enter_context(nc.semaphore(name))

        wq0 = sb("wq0", [P, 2, DC, F])
        wk0 = sb("wk0", [P, 2, DC, F])
        wc0 = sb("wc0", [P, 2, DC, D])
        bq0 = sb("bq0", [P, 2])
        bk0 = sb("bk0", [P, 2])
        wq1 = sb("wq1", [P, DC, D])
        wk1 = sb("wk1", [P, DC, D])
        wv1 = sb("wv1", [P, DC, D])
        wo1 = sb("wo1", [P, DC, D])
        bq1 = sb("bq1", [P, DC])
        bk1 = sb("bk1", [P, DC])
        bv1 = sb("bv1", [P, D])
        bo1 = sb("bo1", [P, D])
        gain = sb("gain", [P, 3, D])
        shift = sb("shift", [P, 3, D])
        ident = sb("ident", [P, P])
        minus_half = sb("minus_half", [P, NT])
        x0 = sb("x0", [P, NT, D])
        x1 = sb("x1", [P, NT, D])
        x2 = sb("x2", [P, NT, D])
        xres = sb("xres", [P, NT, D])
        adj_t = sb("adj_t", [P, NT, N], i32)
        mask_a0 = sb("mask_a0", [P, NT, N], bf16)
        mask_a1 = sb("mask_a1", [P, NT, N], bf16)
        mask_h = sb("mask_h", [P, NT, N], bf16)
        xt = sb("xt", [P, DC, N])
        qt0 = sb("qt0", [P, N])
        kt0 = sb("kt0", [P, N])
        ctxt = sb("ctxt", [P, DC, N])
        pt_l = sb("pt_l", [P, NT, N])
        y_l = sb("y_l", [P, NT, D])
        xt2 = sb("xt2", [P, DC, N])
        parts = sb("parts", [P, DC, 4, N], fp16)
        stack = sb("stack", [P, H, 2, N], fp16)
        v1 = sb("v1", [P, NT, D])
        pt_h = sb("pt_h", [P, 4, NT, N])
        rb = sb("rb", [P, N])
        ot = sb("ot", [P, 2, N])
        y_f = sb("y_f", [P, NT, D])
        xout = sb("xout", [P, NT, D])
        masked_s = sb("masked_s", [P, 4, N])
        probs = sb("probs", [P, 4, N])
        nm_l = sb("nm_l", [P, 2, NT])
        nm_h = sb("nm_h", [P, H, NT])
        sum_l = sb("sum_l", [P, 2, NT])
        sum_h = sb("sum_h", [P, H, NT])
        rinv_l = sb("rinv_l", [P, NT])
        r_l = sb("r_l", [P, NT])
        sum_f = sb("sum_f", [P, 4, NT])
        r_h = sb("r_h", [P, 4, NT])
        r_wide = sb("r_wide", [P, NT, 4, HD])
        stats = {s: sb(f"stats_{s}", [P, NT, 6]) for s in "LF"}
        moments = {s: sb(f"moments_{s}", [P, NT, 2]) for s in "LF"}
        minus_mean = {s: sb(f"minus_mean_{s}", [P, NT]) for s in "LF"}
        var_eps = {s: sb(f"var_eps_{s}", [P, NT]) for s in "LF"}
        rstd = {s: sb(f"rstd_{s}", [P, NT]) for s in "LF"}
        y_norm = sb("y_norm", [P, NT, D])

        ps_s = [ctx.enter_context(nc.psum_tensor(f"ps_s{n}", [P, N], fp32)) for n in range(2)]
        ps_t = [ctx.enter_context(nc.psum_tensor(f"ps_t{n}", [P, NT, P], fp32)) for n in range(2)]
        ps_j = [[ctx.enter_context(nc.psum_tensor(f"ps_j{a}{h}", [P, N], fp32)) for h in range(2)]
                for a in range(2)]
        bounce = nc.dram_tensor("bounce", [DC, 4, HD, 4, N], fp16).ap()

        weights_in = sem("weights_in")
        ident_zero, ident_in, half_in = sem("ident_zero"), sem("ident_in"), sem("half_in")
        x_in, adj_in = sem("x_in"), sem("adj_in")
        mask0_ready, mask1_ready, maskh_ready = sem("mask0_ready"), sem("mask1_ready"), sem("maskh_ready")
        scores_done, masked, exps = sem("scores_done"), sem("masked"), sem("exps")
        transposed, copied_act, copied_dve = sem("transposed"), sem("copied_act"), sem("copied_dve")
        done = {j: sem(f"{j}_done") for j in
                ("X", "QK", "AV", "WC", "X2", "Q", "K", "V", "O", "RB", "WO")}
        xt_ready, qk_ready, ctx_ready = sem("xt_ready"), sem("qk_ready"), sem("ctx_ready")
        xt2_ready, v_ready = sem("xt2_ready"), sem("v_ready")
        hi_ready = {j: sem(f"{j}_hi_ready") for j in "QK"}
        lo_ready = {j: sem(f"{j}_lo_ready") for j in "QK"}
        bounced = [sem(f"bounced{c}") for c in range(DC)]
        stacked = [sem(f"stacked{c}") for c in range(DC)]
        rinv_ready, r_l_ready = sem("rinv_ready"), sem("r_l_ready")
        sum_f_ready, r_h_ready, r_wide_ready = sem("sum_f_ready"), sem("r_h_ready"), sem("r_wide_ready")
        rb_ready, ot_ready = sem("rb_ready"), sem("ot_ready")
        y_ready = {s: sem(f"y_ready_{s}") for s in "LF"}
        stats_ready = {s: sem(f"stats_ready_{s}") for s in "LF"}
        aggregated = {s: sem(f"aggregated_{s}") for s in "LF"}
        moments_ready = {s: sem(f"moments_ready_{s}") for s in "LF"}
        rstd_ready = {s: sem(f"rstd_ready_{s}") for s in "LF"}
        normed = {s: sem(f"normed_{s}") for s in "LF"}
        gained = {s: sem(f"gained_{s}") for s in "LF"}
        ln_done = {s: sem(f"ln_done_{s}") for s in "LF"}
        xres_ready, out_stored = sem("xres_ready"), sem("out_stored")

        waits_passed = sem("waits_passed")


        FIRST = 2

        N_WEIGHTS_IN = 2 * 3 + 4 + 4 + 2 + 2 * 3

        def slots_before(i):
            return PRO_SLOTS + len(LOOP_SLOTS) * i

        def copied(q, r):
            if r == DVE_TILE:
                return copied_dve, q + 1
            return copied_act, q * (NT - 1) + r + 1

        def early(count, n):
            return isinstance(count, int) and count < n

        def settle(eng):
            eng.sem_inc(waits_passed, 1)

        def program(walk, loop):
            first, second, third = PRO_JOBS
            walk(block(0, [("L", 0, 0)], pre=first))
            walk(block(1, [("L", 1, 0)], pre=second, last=first))
            walk(block(2, [("L", 0, 1)], pre=third, last=second, after=0))
            with loop(0, LOOPS) as i:
                graph_of = {"i": i, "i+1": i + 1, "i+2": i + 2}
                slots = [(kind, n, graph_of[g]) for kind, n, g in LOOP_SLOTS]
                jobs = [(name, pair, graph_of[g], l, steps) for name, pair, g, l, steps in LOOP_JOBS]
                last = [(name, pair, i - 1, l) for name, pair, _, l, _ in LOOP_JOBS[-2:]]
                walk(block(slots_before(i), slots, jobs=jobs, last=last, before=True, after=i + 1))
            b = NB - 1
            jobs = [(name, pair, b, l, steps) for name, pair, l, steps in TAIL_JOBS]
            last = [(name, pair, b - 1, l) for name, pair, _, l, _ in LOOP_JOBS[-2:]]
            walk(block(slots_before(LOOPS), [(kind, n, b) for kind, n in TAIL_SLOTS], jobs=jobs,
                       last=last, before=True))

        class block:

            def __init__(self, q0, slots, pre=(), jobs=(), last=(), before=False, after=None):
                self.q0, self.slots, self.before, self.after = q0, slots, before, after
                self.n = len(slots) * NT
                in_bank = {pair: (name, b, l) for name, pair, b, l in last}
                self.pre, self.jobs = [], {}
                for name, pair, b, l in pre:
                    self.pre += [(name, pair, b, l, half, in_bank.get(pair)) for half in range(2)]
                    in_bank[pair] = (name, b, l)
                for name, pair, b, l, steps in jobs:
                    for half, k in enumerate(steps):
                        self.jobs.setdefault(k, []).append((name, pair, b, l, half, in_bank.get(pair)))
                    in_bank[pair] = (name, b, l)

            def tile(self, k):
                s, r = k // NT, k % NT
                if s < len(self.slots):
                    return (self.q0 + s, r, *self.slots[s])
                return None if self.after is None else (self.q0 + s, r, "H", 0, self.after)

            def tiles_at(self, k, ahead):
                first = not self.before and k == 0
                ks = range(0 if first else k + ahead, k + ahead + 1)
                return [t for t in map(self.tile, ks) if t is not None]

            def last_head_slot(self, g):
                return self.q0 + [s[:2] for s in self.slots].index(("H", 4 * g + 3))

            def av_slot(self, l):
                kinds = [s[:2] for s in self.slots]
                if l == 1 and len(kinds) > 1:
                    return self.q0 + kinds.index(("L", 1))
                return self.q0 - 1

            def late_jobs(self, k):
                got = list(self.jobs.get(k - 1, ()))
                return got + (list(self.jobs.get(k, ())) if k >= self.n - 1 else [])

        bl = nc.Block()
        blk = ctx.enter_context(bl)

        @blk.sync
        def _(sp):
            sp.dma_start(x0[:], x_v[0]).then_inc(x_in, 16)
            sp.dma_start(adj_t[:], adj_v[0]).then_inc(adj_in, 16)
            for l in range(2):
                sp.dma_start(wq0[:, l], l0["Wq"][l].rearrange("(c p) f -> p c f", p=P)).then_inc(weights_in, 16)
                sp.dma_start(wk0[:, l], l0["Wk"][l].rearrange("(c p) f -> p c f", p=P)).then_inc(weights_in, 16)
                sp.dma_start(wc0[:, l], l0["Wc"][l].rearrange("(c p) e -> p c e", p=P)).then_inc(weights_in, 16)
            for dst, src in ((bq0, l0["bq"]), (bk0, l0["bk"]), (bq1, l1["bq"]), (bk1, l1["bk"])):
                sp.dma_start(dst[:], src).then_inc(weights_in, 16)
            for dst, src in ((wq1, l1["Wq"]), (wk1, l1["Wk"]), (wv1, l1["Wv"]), (wo1, l1["Wo"])):
                sp.dma_start(dst[:], src.rearrange("(c p) e -> p c e", p=P)).then_inc(weights_in, 16)
            for dst, src in ((bv1, l1["bv"]), (bo1, l1["bo"])):
                sp.dma_start(dst[:], src.partition_broadcast(P)).then_inc(weights_in, 16)
            for n, (g, s) in enumerate(((l0["g"][0], l0["b"][0]), (l0["g"][1], l0["b"][1]), (l1["g"], l1["b"]))):
                sp.dma_start(gain[:, n], g.partition_broadcast(P)).then_inc(weights_in, 16)
                sp.dma_start(shift[:, n], s.partition_broadcast(P)).then_inc(weights_in, 16)

            def load_adj(b, at):
                sp.wait_ge(mask0_ready, b)
                settle(sp)
                sp.dma_start(adj_t[:], adj_v[at]).then_inc(adj_in, 16)

            def load_x(b, at):
                sp.wait_ge(y_ready["L"], 2 * (2 * (b - 1) + 1))
                settle(sp)
                sp.dma_start(x0[:], x_v[at]).then_inc(x_in, 16)

            def copy_mask1(b):
                if not early(b, 1):
                    sp.wait_ge(maskh_ready, 16 * b)
                    settle(sp)
                sp.wait_ge(mask0_ready, b + 1)
                settle(sp)
                sp.dma_start(mask_a1[:], mask_a0[:]).then_inc(mask1_ready, 16)

            def copy_maskh(b, tiles):
                if not early(tiles, 1):
                    sp.wait_ge(masked, tiles)
                    settle(sp)
                sp.wait_ge(mask1_ready, 16 * (b + 1))
                settle(sp)
                sp.dma_start(mask_h[:], mask_a1[:]).then_inc(maskh_ready, 16)

            def stack_parts(c, b, tiles):
                for j in "QK":
                    sp.wait_ge(hi_ready[j], DC * b + c + 1)
                    settle(sp)
                    sp.wait_ge(lo_ready[j], DC * b + c + 1)
                    settle(sp)
                sp.dma_start(bounce[c].rearrange("g d a n -> (g d) a n"), parts[:, c]).then_inc(bounced[c], 16)
                sp.wait_ge(bounced[c], 16 * (b + 1))
                settle(sp)
                if not early(tiles, 1):
                    sp.wait_ge(scores_done, tiles)
                    settle(sp)
                for s in range(4):
                    qa, ka = s // 2, 2 + s % 2
                    for dst, a in ((0, qa), (1, ka)):
                        sp.dma_start(stack[HD * s:HD * s + HD, 4 * c:4 * c + 4, dst, :],
                                     bounce[c, :, :, a, :].rearrange("g d n -> d g n")).then_inc(stacked[c], 16)

            load_adj(1, 1)
            copy_mask1(0)
            load_x(1, 1)
            copy_maskh(0, 2 * NT)
            copy_mask1(1)
            stack_parts(0, 0, 0)
            stack_parts(1, 0, 0)
            with sp.Fori(0, LOOPS) as i:
                q0 = slots_before(i)
                at = (i + 2) % NB
                load_adj(i + 2, at)
                load_x(i + 2, at)
                stack_parts(0, i + 1, (q0 + 4) * NT)
                copy_maskh(i + 1, (q0 + 9) * NT)
                stack_parts(1, i + 1, (q0 + 9) * NT)
                copy_mask1(i + 2)
            sp.wait_ge(mask1_ready, 16 * (NB + 1))
            settle(sp)

        @blk.gpsimd
        def _(pool):
            pool.sem_inc(ln_done["F"], FIRST)
            pool.memset(ident[:], 1.0).then_inc(ident_zero, 1)
            pool.memset(minus_half[:], -0.5).then_inc(half_in, 1)
            pool.wait_ge(ident_zero, 1)
            pool.affine_select(out=ident[:], in_=ident[:], compare_op=ALU.is_equal, fill=0.0, base=0,
                               pattern=[[-1, P]], channel_multiplier=1).then_inc(ident_in, 1)

            def make_mask(b, tiles):
                pool.wait_ge(adj_in, 16 * (b + 1))
                if not early(tiles, 1):
                    pool.wait_ge(masked, tiles)
                if not early(b, 1):
                    pool.wait_ge(mask1_ready, 16 * b)
                settle(pool)
                pool.tensor_scalar(mask_a0[:], adj_t[:], 0.0, MASKED, ALU.is_equal, ALU.mult)\
                    .then_inc(mask0_ready, 1)

            def layer_norm(s, c, y, norm, dst):
                pool.wait_ge(moments_ready[s], c + 1)
                pool.tensor_tensor(rstd[s][:], var_eps[s][:], minus_half[:], ALU.pow).then_inc(rstd_ready[s], 1)
                pool.wait_ge(rstd_ready[s], c + 1)
                settle(pool)
                for t in range(NT):
                    last = pool.tensor_scalar(y_norm[:, t], y[:, t], minus_mean[s][:, t:t + 1],
                                              rstd[s][:, t:t + 1], ALU.add, ALU.mult)
                last.then_inc(normed[s], 1)
                pool.wait_ge(normed[s], c + 1)
                g = gain[:, norm:norm + 1, :].to_broadcast([P, NT, D])
                h = shift[:, norm:norm + 1, :].to_broadcast([P, NT, D])
                pool.tensor_tensor(y_norm[:], y_norm[:], g, ALU.mult).then_inc(gained[s], 1)
                pool.wait_ge(gained[s], c + 1)
                pool.tensor_tensor(dst[:], y_norm[:], h, ALU.add).then_inc(ln_done[s], 1)

            def residual(b):
                pool.wait_ge(y_ready["F"], FIRST + 2 * b)
                pool.wait_ge(ln_done["L"], 2 * b + 2)
                pool.tensor_tensor(xres[:], x2[:], bo1[:].unsqueeze(1).to_broadcast([P, NT, D]), ALU.add)\
                    .then_inc(xres_ready, 1)

            def finish(b):
                layer_norm("F", b, y_f, 2, xout)
                pool.wait_ge(ln_done["F"], FIRST + b + 1)
                pool.dma_start(out_v[b], xout[:]).then_inc(out_stored, 16)
                pool.wait_ge(out_stored, 16 * (b + 1))

            make_mask(0, 0)
            pool.wait_ge(weights_in, 16 * N_WEIGHTS_IN)
            make_mask(1, NT)
            layer_norm("L", 0, y_l, 0, x1)
            layer_norm("L", 1, y_l, 1, x2)
            with pool.Fori(0, LOOPS) as i:
                residual(i)
                layer_norm("L", 2 * (i + 1), y_l, 0, x1)
                make_mask(i + 2, slots_before(i) * NT)
                layer_norm("L", 2 * (i + 1) + 1, y_l, 1, x2)
                finish(i)
            residual(NB - 1)
            finish(NB - 1)

        @blk.tensor
        def _(pe):
            def bank(pair, half, before):
                name, b, l = before or (None, None, None)
                if name == "X":
                    pe.wait_ge(xt_ready, 2 * (2 * b + l) + half + 1)
                if name == "QK":
                    pe.wait_ge(qk_ready, 2 * (2 * b + l) + half + 1)
                if name == "AV":
                    pe.wait_ge(ctx_ready, 2 * (2 * b + l) + half + 1)
                if name == "WC":
                    pe.wait_ge(y_ready["L"], 2 * (2 * b + l) + half + 1)
                if name == "X2":
                    pe.wait_ge(xt2_ready, 2 * b + half + 1)
                if name in ("Q", "K"):
                    pe.wait_ge(lo_ready[name], 2 * b + half + 1)
                if name == "V":
                    pe.wait_ge(v_ready, 2 * b + half + 1)
                if name == "OG":
                    pe.wait_ge(rb_ready if half else ot_ready, FIRST + 2 * b + l + 1)
                if name == "WO":
                    pe.wait_ge(y_ready["F"], FIRST + 2 * b + half + 1)
                return ps_j[pair][half]

            def scores(q, r, kind, n, b):
                n_tile = NT * q + r
                if not early(n_tile, 2):
                    pe.wait_ge(masked, n_tile - 1)
                if kind == "L":
                    if r == 0:
                        pe.wait_ge(qk_ready, 2 * (2 * b + n) + 2)
                    lhs, rhs = qt0[:, r * P:(r + 1) * P], kt0[:]
                else:
                    if r == 0 and n % 4 == 0:
                        pe.wait_ge(stacked[n // 4], 16 * 8 * (b + 1))
                    lhs, rhs = stack[:, n, 0, r * P:(r + 1) * P], stack[:, n, 1, :]
                pe.matmul(ps_s[r % 2][:], lhs, rhs, start=True, stop=True).then_inc(scores_done, 1)

            def transposes(q, r, kind, n, b):
                pe.wait_ge(exps, NT * q + r + 1)
                if not early(NT * q + r, 2):
                    pe.wait_ge(*(copied(q, r - 2) if r >= 2 else copied(q - 1, r + 2)))
                for t in range(NT):
                    last = pe.transpose(ps_t[r % 2][:, t], probs[:, r, t * P:(t + 1) * P], ident[:])
                last.then_inc(transposed, 1)

            def job(name, pair, b, l, half, before, blk_):
                L = 2 * b + l
                if name == "X":
                    if l == 0:
                        pe.wait_ge(x_in, 16 * (b + 1))
                    else:
                        pe.wait_ge(ln_done["L"], 2 * b + 1)
                    src = x1 if l else x0
                    out_bank = bank(pair, half, before)
                    for t in range(NT):
                        last = pe.transpose(out_bank[:, t * P:(t + 1) * P], src[:, t, half * P:(half + 1) * P], ident[:])
                    last.then_inc(done["X"], 1)
                if name == "X2":
                    pe.wait_ge(ln_done["L"], 2 * b + 2)
                    out_bank = bank(pair, half, before)
                    for t in range(NT):
                        last = pe.transpose(out_bank[:, t * P:(t + 1) * P], x2[:, t, half * P:(half + 1) * P], ident[:])
                    last.then_inc(done["X2"], 1)
                if name == "QK":
                    pe.wait_ge(xt_ready, 2 * L + 2)
                    out_bank = bank(pair, half, before)
                    w = (wq0, wk0)[half]
                    for c in range(DC):
                        last = pe.matmul(out_bank[:], w[:, l, c], xt[:, c], start=c == 0, stop=c == DC - 1)
                    last.then_inc(done["QK"], 1)
                if name == "AV":
                    for tile in (DVE_TILE, LAST_ACT_TILE):
                        pe.wait_ge(*copied(blk_.av_slot(l), tile))
                    src = x1 if l else x0
                    out_bank = bank(pair, half, before)
                    for t in range(NT):
                        last = pe.matmul(out_bank[:], src[:, t, half * P:(half + 1) * P], pt_l[:, t],
                                         start=t == 0, stop=t == NT - 1)
                    last.then_inc(done["AV"], 1)
                if name == "WC":
                    pe.wait_ge(ctx_ready, 2 * L + 2)
                    out_bank = bank(pair, half, before)
                    for t in range(2):
                        at = (2 * half + t) * P
                        for c in range(DC):
                            last = pe.matmul(out_bank[:, t * D:(t + 1) * D], ctxt[:, c, at:at + P], wc0[:, l, c],
                                             start=c == 0, stop=c == DC - 1)
                    last.then_inc(done["WC"], 1)
                if name in "QK" and len(name) == 1:
                    pe.wait_ge(xt2_ready, 2 * b + 2)
                    out_bank = bank(pair, half, before)
                    w = {"Q": wq1, "K": wk1}[name]
                    for c in range(DC):
                        last = pe.matmul(out_bank[:], w[:, c, half * P:(half + 1) * P], xt2[:, c],
                                         start=c == 0, stop=c == DC - 1)
                    last.then_inc(done[name], 1)
                if name == "V":
                    pe.wait_ge(xt2_ready, 2 * b + 2)
                    out_bank = bank(pair, half, before)
                    for t in range(2):
                        at = (2 * half + t) * P
                        for c in range(DC):
                            last = pe.matmul(out_bank[:, t * D:(t + 1) * D], xt2[:, c, at:at + P], wv1[:, c],
                                             start=c == 0, stop=c == DC - 1)
                    last.then_inc(done["V"], 1)
                if name == "OG":
                    g = l
                    if half == 0:
                        for tile in (DVE_TILE, LAST_ACT_TILE):
                            pe.wait_ge(*copied(blk_.last_head_slot(g), tile))
                        pe.wait_ge(v_ready, 2 * b + 2)
                        out_bank = bank(pair, half, before)
                        for t in range(NT):
                            for h in range(4):
                                col = (4 * g + h) * HD
                                last = pe.matmul(out_bank[h * HD:(h + 1) * HD, :], v1[:, t, col:col + HD],
                                                 pt_h[:, h, t], start=t == 0, stop=t == NT - 1)
                        last.then_inc(done["O"], 1)
                    else:
                        pe.wait_ge(r_wide_ready, 2 * b + g + 1)
                        out_bank = bank(pair, half, before)
                        for t in range(NT):
                            last = pe.transpose(out_bank[:, t * P:(t + 1) * P],
                                                r_wide[:, t].rearrange("p h d -> p (h d)"), ident[:])
                        last.then_inc(done["RB"], 1)
                if name == "WO":
                    pe.wait_ge(ot_ready, FIRST + 2 * b + 2)
                    out_bank = bank(pair, half, before)
                    for t in range(2):
                        at = (2 * half + t) * P
                        for g in range(2):
                            last = pe.matmul(out_bank[:, t * D:(t + 1) * D], ot[:, g, at:at + P], wo1[:, g],
                                             start=g == 0, stop=g == 1)
                    last.then_inc(done["WO"], 1)

            def walk(b_):
                for j in b_.pre:
                    job(*j, b_)
                for k in range(b_.n):
                    ahead = b_.tiles_at(k, AHEAD)
                    if k == 0 and not b_.before:
                        for t in ahead:
                            scores(*t)
                        ahead = []
                    transposes(*b_.tile(k))
                    for t in ahead:
                        scores(*t)
                    for j in b_.jobs.get(k, ()):
                        job(*j, b_)

            pe.sem_inc(done["RB"], FIRST)
            pe.wait_ge(ident_in, 1)
            pe.wait_ge(weights_in, 16 * N_WEIGHTS_IN)
            program(walk, pe.Fori)

        @blk.scalar
        def _(act):
            def exp(q, r, kind, n, b):
                tile = NT * q + r
                act.wait_ge(masked, tile + 1)
                if not early(tile, 4):
                    act.wait_ge(transposed, tile - 3)
                nm, total = (nm_l, sum_l) if kind == "L" else (nm_h, sum_h)
                act.activation(probs[:, r], masked_s[:, r], ACT.Exp, bias=nm[:, n, r:r + 1], scale=-1.0,
                               accum_out=total[:, n, r:r + 1]).then_inc(exps, 1)

            def copy_tile(q, r, kind, n, b):
                act.wait_ge(transposed, NT * q + r + 1)
                dst = (pt_l if kind == "L" else pt_h[:, n % 4])[:, :, r * P:(r + 1) * P]
                act.activation(dst, ps_t[r % 2][:], ACT.Copy).then_inc(copied_act, 1)

            def job(name, pair, b, l, half, before, blk_):
                L = 2 * b + l
                if pair is None:
                    return
                bank = ps_j[pair][half][:]
                if name == "X":
                    act.wait_ge(done["X"], 2 * L + half + 1)
                    act.activation(xt[:, half], bank, ACT.Copy).then_inc(xt_ready, 1)
                if name == "X2":
                    act.wait_ge(done["X2"], 2 * b + half + 1)
                    act.activation(xt2[:, half], bank, ACT.Copy).then_inc(xt2_ready, 1)
                if name == "QK":
                    act.wait_ge(done["QK"], 2 * L + half + 1)
                    dst, bias = ((qt0, bq0), (kt0, bk0))[half]
                    act.activation(dst[:], bank, ACT.Identity, bias=bias[:, l:l + 1]).then_inc(qk_ready, 1)
                if name == "AV":
                    act.wait_ge(done["AV"], 2 * L + half + 1)
                    act.activation(ctxt[:, half], bank, ACT.Copy).then_inc(ctx_ready, 1)
                if name in "QK" and len(name) == 1:
                    act.wait_ge(done[name], DC * b + half + 1)
                    if not early(b, 1):
                        act.wait_ge(bounced[half], 16 * b)
                    a, bias = {"Q": (0, bq1), "K": (2, bk1)}[name]
                    act.activation(parts[:, half, a], bank, ACT.Identity, bias=bias[:, half:half + 1])\
                        .then_inc(hi_ready[name], 1)
                if name == "OG" and half == 1:
                    g = l
                    act.wait_ge(done["RB"], FIRST + 2 * b + g + 1)
                    act.wait_ge(ot_ready, FIRST + 2 * b + g)
                    act.activation(rb[:], bank, ACT.Copy).then_inc(rb_ready, 1)

            def walk(b_):
                for j in b_.pre:
                    job(*j, b_)
                for k in range(b_.n):
                    for t in b_.tiles_at(k, 1):
                        exp(*t)
                    copy_now(b_, k)
                    for j in b_.late_jobs(k):
                        job(*j, b_)

            def copy_now(b_, k):
                t = b_.tile(k)
                if t[1] != DVE_TILE:
                    copy_tile(*t)

            act.sem_inc(rb_ready, FIRST)
            act.wait_ge(weights_in, 16 * N_WEIGHTS_IN)
            program(walk, act.Fori)

        @blk.vector
        def _(dve):
            def mask(q, r, kind, n, b):
                tile = NT * q + r
                dve.wait_ge(scores_done, tile + 1)
                if not early(tile, 4):
                    dve.wait_ge(exps, tile - 3)
                if kind == "L":
                    if r == 0:
                        dve.wait_ge(*((mask1_ready, 16 * (b + 1)) if n else (mask0_ready, b + 1)))
                    m, nm, scale = (mask_a0, mask_a1)[n], nm_l, L0_SCALE
                else:
                    if r == 0 and n == 0:
                        dve.wait_ge(maskh_ready, 16 * (b + 1))
                    m, nm, scale = mask_h, nm_h, L1_SCALE
                settle(dve)
                dve.tensor_tensor_reduce(out=masked_s[:, r], in0=ps_s[r % 2][:], in1=m[:, r], scale=-scale,
                                         scalar=BIG, op0=ALU.add, op1=ALU.min,
                                         accum_out=nm[:, n, r:r + 1]).then_inc(masked, 1)

            def copy_tile(q, r, kind, n, b):
                dve.wait_ge(transposed, NT * q + r + 1)
                dst = (pt_l if kind == "L" else pt_h[:, n % 4])[:, :, r * P:(r + 1) * P]
                dve.tensor_copy(dst, ps_t[r % 2][:]).then_inc(copied_dve, 1)

            def statistics(s, c, y, half):
                dve.wait_ge(y_ready[s], (FIRST if s == "F" else 0) + 2 * c + half + 1)
                for t in range(2 * half, 2 * half + 2):
                    last = dve.bn_stats(stats[s][:, t], y[:, t])
                last.then_inc(stats_ready[s], 1)
                if half == 1:
                    dve.wait_ge(stats_ready[s], 2 * c + 2)
                    settle(dve)
                    for t in range(NT):
                        last = dve.bn_aggr(moments[s][:, t], stats[s][:, t])
                    last.then_inc(aggregated[s], 1)
                    dve.wait_ge(aggregated[s], c + 1)
                    dve.tensor_scalar(minus_mean[s][:], moments[s][:, :, 0], -1.0, None, ALU.mult)
                    dve.tensor_scalar(var_eps[s][:], moments[s][:, :, 1], LN_EPS, None, ALU.add)\
                        .then_inc(moments_ready[s], 1)

            def job(name, pair, b, l, half, before, blk_):
                L = 2 * b + l
                if name == "R":
                    g = l
                    G = 2 * b + g
                    dve.wait_ge(exps, NT * (blk_.last_head_slot(g) + 1))
                    heads = slice(4 * g, 4 * g + 4)
                    dve.scalar_tensor_tensor(sum_f[:], nm_h[:, heads], ALL_MASKED, sum_h[:, heads],
                                             ALU.is_lt, ALU.mult).then_inc(sum_f_ready, 1)
                    dve.wait_ge(sum_f_ready, G + 1)
                    dve.reciprocal(r_h[:], sum_f[:]).then_inc(r_h_ready, 1)
                    dve.wait_ge(r_h_ready, G + 1)
                    dve.wait_ge(done["RB"], FIRST + G)
                    dve.tensor_copy(r_wide[:].rearrange("p t h d -> p h t d"),
                                    r_h[:].unsqueeze(3).to_broadcast([P, 4, NT, HD]))\
                        .then_inc(r_wide_ready, 1)
                    return
                bank = ps_j[pair][half][:]
                two = bank.rearrange("p (t d) -> p t d", t=2)
                nts = slice(2 * half, 2 * half + 2)
                if name == "WC":
                    if half == 0:
                        dve.wait_ge(done["WC"], 2 * L + 1)
                        dve.reciprocal(rinv_l[:], sum_l[:, l]).then_inc(rinv_ready, 1)
                        dve.wait_ge(rinv_ready, L + 1)
                        dve.scalar_tensor_tensor(r_l[:], nm_l[:, l], ALL_MASKED, rinv_l[:], ALU.is_lt,
                                                 ALU.mult).then_inc(r_l_ready, 1)
                        dve.wait_ge(r_l_ready, L + 1)
                    dve.wait_ge(done["WC"], 2 * L + half + 1)
                    if not early(L, 1):
                        dve.wait_ge(ln_done["L"], L)
                    if l == 0:
                        dve.wait_ge(x_in, 16 * (b + 1))
                    src = x1 if l else x0
                    for t in range(2):
                        nt = 2 * half + t
                        last = dve.scalar_tensor_tensor(y_l[:, nt], two[:, t], r_l[:, nt:nt + 1], src[:, nt],
                                                        ALU.mult, ALU.add)
                    last.then_inc(y_ready["L"], 1)
                    statistics("L", L, y_l, half)
                if name in "QK" and len(name) == 1:
                    dve.wait_ge(hi_ready[name], DC * b + half + 1)
                    a, bias = {"Q": (0, bq1), "K": (2, bk1)}[name]
                    dve.scalar_tensor_tensor(parts[:, half, a + 1], bank, bias[:, half:half + 1],
                                             parts[:, half, a], ALU.add, ALU.subtract)\
                        .then_inc(lo_ready[name], 1)
                if name == "V":
                    dve.wait_ge(done["V"], 2 * b + half + 1)
                    dve.tensor_tensor(v1[:, nts], two, bv1[:].unsqueeze(1).to_broadcast([P, 2, D]), ALU.add)\
                        .then_inc(v_ready, 1)
                if name == "OG" and half == 1:
                    g = l
                    dve.wait_ge(done["O"], 2 * b + g + 1)
                    dve.wait_ge(rb_ready, FIRST + 2 * b + g + 1)
                    dve.tensor_tensor(ot[:, g], ps_j[pair][0][:], rb[:], ALU.mult).then_inc(ot_ready, 1)
                if name == "WO":
                    dve.wait_ge(done["WO"], 2 * b + half + 1)
                    dve.wait_ge(xres_ready, b + 1)
                    dve.wait_ge(ln_done["F"], FIRST + b)
                    dve.tensor_tensor(y_f[:, nts], two, xres[:, nts], ALU.add).then_inc(y_ready["F"], 1)
                    statistics("F", b, y_f, half)

            def walk(b_):
                for j in b_.pre:
                    job(*j, b_)
                for k in range(b_.n):
                    for t in b_.tiles_at(k, 2):
                        mask(*t)
                    t = b_.tile(k)
                    if t[1] == DVE_TILE:
                        copy_tile(*t)
                    for j in b_.late_jobs(k):
                        job(*j, b_)

            dve.sem_inc(y_ready["F"], FIRST)
            dve.sem_inc(ot_ready, FIRST)
            dve.wait_ge(weights_in, 16 * N_WEIGHTS_IN)
            program(walk, dve.Fori)


def kernel(**inputs):
    import numpy as _np
    import concourse.bacc as _bacc
    from concourse import mybir as _mybir
    from concourse.bass_utils import run_bass_kernel_spmd as _run

    nc = _bacc.Bacc("TRN2", target_bir_lowering=False, num_devices=1)
    arrays = {}

    def dram(name, a):
        a = _np.ascontiguousarray(a)
        arrays[name] = a
        return nc.dram_tensor(name, a.shape, _mybir.dt.from_np(a.dtype), kind="ExternalInput").ap()

    def arr(name):
        return _np.asarray(inputs[name])

    x = dram("x_dram", arr("x"))
    adj = dram("adj_dram", arr("adj"))
    l0 = {
        "Wq": dram("l0_wq", arr("L0_gnn_Wq").transpose(0, 2, 1)),
        "Wk": dram("l0_wk", arr("L0_gnn_Wk").transpose(0, 2, 1)),
        "Wc": dram("l0_wc", arr("L0_gnn_Wc").transpose(0, 2, 1)),
        "bq": dram("l0_bq", arr("L0_gnn_bq").T),
        "bk": dram("l0_bk", arr("L0_gnn_bk").T),
        "g": dram("l0_g", arr("L0_gnn_ln_g")),
        "b": dram("l0_b", arr("L0_gnn_ln_b")),
    }
    l1 = {
        "Wq": dram("l1_wq", arr("L1_gnn_Wq")),
        "Wk": dram("l1_wk", arr("L1_gnn_Wk")),
        "Wv": dram("l1_wv", arr("L1_gnn_Wv")),
        "Wo": dram("l1_wo", arr("L1_gnn_Wo")),
        "bq": dram("l1_bq", arr("L1_gnn_bq").reshape(2, 128).T),
        "bk": dram("l1_bk", arr("L1_gnn_bk").reshape(2, 128).T),
        "bv": dram("l1_bv", arr("L1_gnn_bv")),
        "bo": dram("l1_bo", arr("L1_gnn_bo")),
        "g": dram("l1_g", arr("L1_gnn_gamma")),
        "b": dram("l1_b", arr("L1_gnn_beta")),
    }
    out = nc.dram_tensor("out_dram", arrays["x_dram"].shape, _mybir.dt.float32, kind="ExternalOutput").ap()
    graph_attention(nc, x, adj, l0, l1, out)
    r = _run(nc, [arrays], core_ids=[0])
    return r.results[0]["out_dram"]
```

```python
from contextlib import ExitStack

import concourse.bass as bass
from concourse import mybir

P = 128
NB, N, D = 16, 512, 256
F = 128
H, HD = 8, 32
NT = N // P
DC = D // P
LN_EPS = 1e-5
L0_SCALE = float(F) ** -0.5
L1_SCALE = float(HD) ** -0.5
MASKED = -1e30
ALL_MASKED = 1e28
BIG = 3e38

LOOP_SLOTS = [("H", 2, "i"), ("L", 1, "i+1"), ("H", 3, "i"), ("H", 4, "i"), ("H", 5, "i"), ("L", 0, "i+2"),
              ("H", 6, "i"), ("H", 7, "i"), ("H", 0, "i+1"), ("H", 1, "i+1")]
LOOPS = NB - 2
TAIL_SLOTS = ([("H", 2, "i"), ("L", 1, "i+1")] + [("H", h, "i") for h in range(3, 8)]
              + [("H", h, "i+1") for h in range(8)])
PRO_SLOTS = [("L", 0, 1), ("H", 0, 0), ("H", 1, 0)]
AHEAD = 3

LOOP_JOBS = [
    ("V", 1, "i", 0, (0, 1)), ("X", 0, "i+2", 0, (2, 2)), ("QK", 1, "i+2", 0, (4, 5)),
    ("AV", 0, "i+1", 1, (6, 7, 8, 9)), ("R", None, "i", 0, (11,)), ("OG", 1, "i", 0, (10, 11, 12, 13, 14)),
    ("WC", 0, "i+1", 1, (12, 13)), ("N", None, "i+1", 1, (15,)),
    ("X2", 1, "i+1", 0, (17, 17)), ("Q", 0, "i+1", 0, (19, 21)), ("K", 1, "i+1", 0, (20, 22)),
    ("AV", 0, "i+2", 0, (23, 24, 25, 26)), ("WC", 1, "i+2", 0, (28, 29)), ("N", None, "i+2", 0, (31,)),
    ("R", None, "i", 1, (31,)), ("OG", 0, "i", 1, (30, 31, 32, 33, 34)),
    ("X", 1, "i+2", 1, (34, 34)), ("QK", 1, "i+2", 1, (36, 37)), ("WO", 0, "i", 0, (38, 39)),
]
PRO_BLOCK_JOBS = [
    ("AV", 0, 1, 0, (2, 3, 4, 5)), ("WC", 1, 1, 0, (7, 8)), ("N", None, 1, 0, (9,)),
    ("X", 0, 1, 1, (11, 11)), ("QK", 1, 1, 1, (11, 11)),
]
PRO_JOBS = [
    [("X", 0, 0, 0), ("QK", 1, 0, 0)],
    [("AV", 0, 0, 0), ("WC", 1, 0, 0), ("N", None, 0, 0), ("X", 0, 0, 1), ("QK", 1, 0, 1)],
    [("X", 0, 1, 0), ("AV", 1, 0, 1), ("WC", 0, 0, 1), ("QK", 1, 1, 0), ("N", None, 0, 1),
     ("X2", 0, 0, 0), ("Q", 1, 0, 0), ("K", 0, 0, 0)],
]
TAIL_JOBS = [
    ("V", 1, "i", 0, (0, 1)),
    ("AV", 0, "i+1", 1, (6, 7, 8, 9)), ("R", None, "i", 0, (11,)), ("OG", 1, "i", 0, (10, 11, 12, 13, 14)),
    ("WC", 0, "i+1", 1, (12, 13)), ("N", None, "i+1", 1, (15,)),
    ("X2", 1, "i+1", 0, (17, 17)), ("Q", 0, "i+1", 0, (19, 21)), ("K", 1, "i+1", 0, (20, 22)),
    ("R", None, "i", 1, (27,)), ("OG", 0, "i", 1, (26, 27, 28, 29, 30)),
    ("V", 1, "i+1", 0, (31, 32)), ("WO", 0, "i", 0, (33, 34)),
    ("R", None, "i+1", 0, (43,)), ("OG", 1, "i+1", 0, (42, 43, 44, 45, 46)),
    ("R", None, "i+1", 1, (58,)), ("OG", 1, "i+1", 1, (58, 59, 59, 59, 59)), ("WO", 0, "i+1", 0, (59, 59)),
]
PARTS = {"AV": 4, "OG": 5, "R": 1, "N": 1}
DVE_TILE = 3
LAST_ACT_TILE = 2


def graph_attention(nc, x, adj, l0, l1, out):
    fp32, fp16, bf16, i32 = mybir.dt.float32, mybir.dt.float16, mybir.dt.bfloat16, mybir.dt.int32
    fp32r = mybir.dt.float32r
    ALU, ACT = mybir.AluOpType, mybir.ActivationFunctionType

    x_v = x.rearrange("b (t p) d -> b p t d", p=P)
    adj_v = adj.rearrange("b (t p) k -> b p t k", p=P)
    out_v = out.rearrange("b (t p) d -> b p t d", p=P)

    ctx = ExitStack()
    with ctx:
        def sb(name, shape, dt=fp32):
            return ctx.enter_context(nc.sbuf_tensor(name, shape, dt))

        def sem(name):
            return ctx.enter_context(nc.semaphore(name))

        wq0 = sb("wq0", [P, 2, 2, DC, F], fp32r)
        wk0 = sb("wk0", [P, 2, 2, DC, F], fp32r)
        wc0 = sb("wc0", [P, 2, 2, DC, D], fp32r)
        wq1 = sb("wq1", [P, 2, DC, D], fp32r)
        wk1 = sb("wk1", [P, 2, DC, D], fp32r)
        wv1 = sb("wv1", [P, 2, DC, D], fp32r)
        wo1 = sb("wo1", [P, DC, D])
        bq0 = sb("bq0", [P, 2])
        bk0 = sb("bk0", [P, 2])
        bq1 = sb("bq1", [P, DC])
        bk1 = sb("bk1", [P, DC])
        gain_c = sb("gain_c", [P, 2, DC])
        shift_c = sb("shift_c", [P, 2, DC])
        bv1 = sb("bv1", [P, D])
        bo1 = sb("bo1", [P, D])
        gain = sb("gain", [P, 3, D])
        shift = sb("shift", [P, 3, D])
        ident = sb("ident", [P, P])
        shift_wide = sb("shift_wide", [P, DC, P])
        minus_half = sb("minus_half", [P, NT])
        x0 = sb("x0", [P, NT, D])
        x1 = sb("x1", [P, NT, D])
        x2 = sb("x2", [P, NT, D])
        adj_t = sb("adj_t", [P, NT, N], i32)
        mask_a0 = sb("mask_a0", [P, NT, N], bf16)
        mask_a1 = sb("mask_a1", [P, NT, N], bf16)
        mask_h = sb("mask_h", [P, NT, N], bf16)
        xt = sb("xt", [P, 2, DC, N], fp32r)
        qt0 = sb("qt0", [P, 2, N], fp32r)
        kt0 = sb("kt0", [P, 2, N], fp32r)
        ctxt = sb("ctxt", [P, 2, DC, N], fp32r)
        pt_l = sb("pt_l", [P, NT, N])
        y_l = sb("y_l", [P, NT, D])
        xt2 = sb("xt2", [P, 2, DC, N], fp32r)
        parts = sb("parts", [P, DC, 4, N], fp16)
        stack = sb("stack", [P, H, 2, N], fp16)
        v1 = sb("v1", [P, NT, D])
        pt_h = sb("pt_h", [P, 4, NT, N])
        rb = sb("rb", [P, N])
        ot = sb("ot", [P, 2, N])
        y_f = sb("y_f", [P, NT, D])
        masked_s = sb("masked_s", [P, 4, N])
        probs = sb("probs", [P, 4, N])
        nm_l = sb("nm_l", [P, 2, NT])
        nm_h = sb("nm_h", [P, H, NT])
        sum_l = sb("sum_l", [P, 2, NT])
        sum_h = sb("sum_h", [P, H, NT])
        rinv_l = sb("rinv_l", [P, NT])
        r_l = sb("r_l", [P, NT])
        sum_f = sb("sum_f", [P, 4, NT])
        r_h = sb("r_h", [P, 4, NT])
        r_wide = sb("r_wide", [P, NT, 4, HD])
        stats = {s: sb(f"stats_{s}", [P, NT, 6]) for s in "LF"}
        moments = {s: sb(f"moments_{s}", [P, NT, 2]) for s in "LF"}
        minus_mean = {s: sb(f"minus_mean_{s}", [P, NT]) for s in "LF"}
        var_eps = {s: sb(f"var_eps_{s}", [P, NT]) for s in "LF"}
        rstd = {s: sb(f"rstd_{s}", [P, NT]) for s in "LF"}

        raw_flat = pt_h[:].rearrange("p h t n -> p (h t n)")
        raw, at = {}, 0
        for name, width in (("wq0", 2 * DC * F), ("wk0", 2 * DC * F), ("wc0", 2 * DC * D),
                            ("wq1", DC * D), ("wk1", DC * D), ("wv1", DC * D)):
            raw[name] = raw_flat[:, at:at + width]
            at += width

        ps_s = [ctx.enter_context(nc.psum_tensor(f"ps_s{n}", [P, N], fp32)) for n in range(2)]
        ps_t = [ctx.enter_context(nc.psum_tensor(f"ps_t{n}", [P, NT, P], fp32)) for n in range(2)]
        ps_j = [[ctx.enter_context(nc.psum_tensor(f"ps_j{a}{h}", [P, N], fp32)) for h in range(2)]
                for a in range(2)]
        bounce = nc.dram_tensor("bounce", [DC, 4, HD, 4, N], fp16).ap()

        weights_in = sem("weights_in")
        ident_zero, ident_in, half_in = sem("ident_zero"), sem("ident_in"), sem("half_in")
        x_in, adj_in = sem("x_in"), sem("adj_in")
        mask0_ready, mask1_ready = sem("mask0_ready"), sem("mask1_ready")
        maskh_ready = [sem(f"maskh{r}_ready") for r in range(NT)]
        scores_done, masked, exps = sem("scores_done"), sem("masked"), sem("exps")
        transposed, copied_act, copied_dve = sem("transposed"), sem("copied_act"), sem("copied_dve")
        done = {j: sem(f"{j}_done") for j in
                ("X", "QK", "AV", "WC", "X2", "Q", "K", "V", "O", "RB", "WO")}
        xt_hi, qk_hi, ctx_hi, xt2_hi = sem("xt_hi"), sem("qk_hi"), sem("ctx_hi"), sem("xt2_hi")
        xt_ready, qk_ready, ctx_ready = sem("xt_ready"), sem("qk_ready"), sem("ctx_ready")
        xt2_ready, v_ready = sem("xt2_ready"), sem("v_ready")
        weights0_in, bias_sums, bias_ready = sem("weights0_in"), sem("bias_sums"), sem("bias_ready")
        scaled, weights_hi, weights_ready = sem("scaled"), sem("weights_hi"), sem("weights_ready")
        hi_ready = {j: sem(f"{j}_hi_ready") for j in "QK"}
        lo_ready = {j: sem(f"{j}_lo_ready") for j in "QK"}
        bounced = [sem(f"bounced{c}") for c in range(DC)]
        stacked = [sem(f"stacked{c}") for c in range(DC)]
        rinv_ready, r_l_ready = sem("rinv_ready"), sem("r_l_ready")
        sum_f_ready, r_h_ready, r_wide_ready = sem("sum_f_ready"), sem("r_h_ready"), sem("r_wide_ready")
        rb_ready, ot_ready = sem("rb_ready"), sem("ot_ready")
        y_ready = {s: sem(f"y_ready_{s}") for s in "LF"}
        stats_ready = {s: sem(f"stats_ready_{s}") for s in "LF"}
        aggregated = {s: sem(f"aggregated_{s}") for s in "LF"}
        moments_ready = {s: sem(f"moments_ready_{s}") for s in "LF"}
        rstd_ready = {s: sem(f"rstd_ready_{s}") for s in "LF"}
        normed = {s: sem(f"normed_{s}") for s in "LF"}
        gained = {s: sem(f"gained_{s}") for s in "LF"}
        ln_done = {s: sem(f"ln_done_{s}") for s in "LF"}
        xres_ready, out_stored = sem("xres_ready"), sem("out_stored")

        waits_passed = sem("waits_passed")


        FIRST = 2

        N_WEIGHTS0_IN = 2 + 2
        N_WEIGHTS_IN = 5 + 4 + 2 + 2 * 3

        def slots_before(i):
            return 2 + len(PRO_SLOTS) + len(LOOP_SLOTS) * i

        def copied(q, r):
            if r == DVE_TILE:
                return copied_dve, q + 1
            return copied_act, q * (NT - 1) + r + 1

        def early(count, n):
            return isinstance(count, int) and count < n

        def settle(eng):
            eng.sem_inc(waits_passed, 1)

        def program(walk, loop):
            first, second, third = PRO_JOBS
            walk(block(0, [("L", 0, 0)], pre=first))
            walk(block(1, [("L", 1, 0)], pre=second, last=first))
            walk(block(2, PRO_SLOTS, pre=third, jobs=PRO_BLOCK_JOBS, last=second, after=("H", 2, 0)))

            def named(rows, i):
                graph_of = {"i": i, "i+1": i + 1, "i+2": i + 2}
                return [tuple(graph_of.get(v, v) if isinstance(v, str) else v for v in row) for row in rows]

            def before_loop_body(i):
                return [("WO", 0, i - 1, 0), ("QK", 1, i + 1, 1)]

            with loop(0, LOOPS) as i:
                walk(block(slots_before(i), named(LOOP_SLOTS, i), jobs=named(LOOP_JOBS, i),
                           last=before_loop_body(i), before=True, after=("H", 2, i + 1)))
            i = LOOPS
            walk(block(slots_before(i), named(TAIL_SLOTS, i), jobs=named(TAIL_JOBS, i),
                       last=before_loop_body(i), before=True))

        class block:

            def __init__(self, q0, slots, pre=(), jobs=(), last=(), before=False, after=None):
                self.q0, self.slots, self.before, self.after = q0, slots, before, after
                self.n = len(slots) * NT
                in_bank = {pair: (name, b, l) for name, pair, b, l in last if pair is not None}
                self.pre, self.jobs = [], {}
                for name, pair, b, l in pre:
                    halves = range(PARTS.get(name, 2))
                    self.pre += [(name, pair, b, l, half, in_bank.get(pair)) for half in halves]
                    in_bank[pair] = (name, b, l)
                for name, pair, b, l, steps in jobs:
                    for half, k in enumerate(steps):
                        self.jobs.setdefault(k, []).append((name, pair, b, l, half, in_bank.get(pair)))
                    in_bank[pair] = (name, b, l)

            def tile(self, k):
                s, r = k // NT, k % NT
                if s < len(self.slots):
                    return (self.q0 + s, r, *self.slots[s])
                return None if self.after is None else (self.q0 + s, r, *self.after)

            def tiles_at(self, k, ahead):
                first = not self.before and k == 0
                ks = range(0 if first else k + ahead, k + ahead + 1)
                return [t for t in map(self.tile, ks) if t is not None]

            def slot_of(self, kind, n, b):
                for s, (kind_, n_, b_) in enumerate(self.slots):
                    same_graph = b is b_ or (isinstance(b, int) and isinstance(b_, int) and b == b_)
                    if (kind_, n_) == (kind, n) and same_graph:
                        return self.q0 + s
                return self.q0 - 1

            def late_jobs(self, k):
                got = list(self.jobs.get(k - 1, ()))
                return got + (list(self.jobs.get(k, ())) if k >= self.n - 1 else [])

        PART_PAIRS = ((0, 0), (0, 1), (1, 0))
        split_weights = [
            ("wq0", lambda a: wq0[:, a].rearrange("p l c f -> p (l c f)")),
            ("wk0", lambda a: wk0[:, a].rearrange("p l c f -> p (l c f)")),
            ("wc0", lambda a: wc0[:, a].rearrange("p l c f -> p (l c f)")),
            ("wq1", lambda a: wq1[:, a].rearrange("p c f -> p (c f)")),
            ("wk1", lambda a: wk1[:, a].rearrange("p c f -> p (c f)")),
            ("wv1", lambda a: wv1[:, a].rearrange("p c f -> p (c f)")),
        ]

        blk = ctx.enter_context(nc.Block())

        @blk.sync
        def _(sp):
            sp.dma_start(x0[:], x_v[0]).then_inc(x_in, 16)
            sp.dma_start(adj_t[:], adj_v[0]).then_inc(adj_in, 16)
            for name, src in (("wq0", l0["Wq"]), ("wk0", l0["Wk"])):
                sp.dma_start(raw[name].rearrange("p (l c f) -> p l c f", l=2, c=DC),
                             src.rearrange("l (c p) f -> p l c f", p=P)).then_inc(weights0_in, 16)
            for dst, src in ((bq0, l0["bq"]), (bk0, l0["bk"])):
                sp.dma_start(dst[:], src).then_inc(weights0_in, 16)
            sp.dma_start(raw["wc0"].rearrange("p (l c f) -> p l c f", l=2, c=DC),
                         l0["Wc"].rearrange("l (c p) f -> p l c f", p=P)).then_inc(weights_in, 16)
            for dst, src in ((raw["wq1"], l1["Wq"]), (raw["wk1"], l1["Wk"]), (raw["wv1"], l1["Wv"]),
                             (wo1[:].rearrange("p c e -> p (c e)"), l1["Wo"])):
                sp.dma_start(dst.rearrange("p (c e) -> p c e", c=DC),
                             src.rearrange("(c p) e -> p c e", p=P)).then_inc(weights_in, 16)
            for dst, src in ((bq1[:], l1["bq"]), (bk1[:], l1["bk"]),
                             (gain_c[:].rearrange("p l c -> p (l c)"), l0["g_c"]),
                             (shift_c[:].rearrange("p l c -> p (l c)"), l0["b_c"])):
                sp.dma_start(dst, src).then_inc(weights_in, 16)
            for dst, src in ((bv1, l1["bv"]), (bo1, l1["bo"])):
                sp.dma_start(dst[:], src.partition_broadcast(P)).then_inc(weights_in, 16)
            for n, (g, s) in enumerate(((l0["g"][0], l0["b"][0]), (l0["g"][1], l0["b"][1]), (l1["g"], l1["b"]))):
                sp.dma_start(gain[:, n], g.partition_broadcast(P)).then_inc(weights_in, 16)
                sp.dma_start(shift[:, n], s.partition_broadcast(P)).then_inc(weights_in, 16)

            def load_adj(b):
                sp.wait_ge(mask0_ready, b)
                settle(sp)
                sp.dma_start(adj_t[:], adj_v[b]).then_inc(adj_in, 16)

            def load_x(b):
                sp.wait_ge(y_ready["L"], 2 * (2 * (b - 1) + 1))
                settle(sp)
                sp.dma_start(x0[:], x_v[b]).then_inc(x_in, 16)

            def copy_mask1(b):
                if not early(b, 1):
                    for r in range(NT):
                        sp.wait_ge(maskh_ready[r], 16 * b)
                        settle(sp)
                sp.wait_ge(mask0_ready, b + 1)
                settle(sp)
                sp.dma_start(mask_a1[:], mask_a0[:]).then_inc(mask1_ready, 16)

            def copy_maskh(b, tiles, each):
                for r in range(NT):
                    sp.wait_ge(masked, tiles + each * (r + 1))
                    settle(sp)
                    sp.wait_ge(mask1_ready, 16 * (b + 1))
                    settle(sp)
                    sp.dma_start(mask_h[:, r], mask_a1[:, r]).then_inc(maskh_ready[r], 16)

            def stack_parts(c, b, tiles):
                for j in "QK":
                    sp.wait_ge(hi_ready[j], DC * b + c + 1)
                    settle(sp)
                    sp.wait_ge(lo_ready[j], DC * b + c + 1)
                    settle(sp)
                sp.dma_start(bounce[c].rearrange("g d a n -> (g d) a n"), parts[:, c]).then_inc(bounced[c], 16)
                sp.wait_ge(bounced[c], 16 * (b + 1))
                settle(sp)
                if not early(tiles, 1):
                    sp.wait_ge(scores_done, tiles)
                    settle(sp)
                for s in range(4):
                    qa, ka = s // 2, 2 + s % 2
                    for dst, a in ((0, qa), (1, ka)):
                        sp.dma_start(stack[HD * s:HD * s + HD, 4 * c:4 * c + 4, dst, :],
                                     bounce[c, :, :, a, :].rearrange("g d n -> d g n")).then_inc(stacked[c], 16)

            load_adj(1)
            copy_mask1(0)
            load_x(1)
            copy_maskh(0, 2 * NT, 0)
            copy_mask1(1)
            stack_parts(0, 0, 0)
            stack_parts(1, 0, 0)
            with sp.Fori(0, LOOPS) as i:
                q0 = slots_before(i)
                load_x(i + 2)
                load_adj(i + 2)
                stack_parts(0, i + 1, (q0 + 3) * NT)
                copy_maskh(i + 1, (q0 + 7) * NT, 1)
                copy_mask1(i + 2)
                stack_parts(1, i + 1, (q0 + 8) * NT)
            q0 = slots_before(LOOPS)
            stack_parts(0, LOOPS + 1, (q0 + 3) * NT)
            copy_maskh(LOOPS + 1, (q0 + 6) * NT, 1)
            stack_parts(1, LOOPS + 1, (q0 + 7) * NT)

        @blk.gpsimd
        def _(pool):
            pool.memset(ident[:], 1.0).then_inc(ident_zero, 1)
            pool.memset(minus_half[:], -0.5).then_inc(half_in, 1)
            pool.wait_ge(ident_zero, 1)
            pool.affine_select(out=ident[:], in_=ident[:], compare_op=ALU.is_equal, fill=0.0, base=0,
                               pattern=[[-1, P]], channel_multiplier=1).then_inc(ident_in, 1)

            def make_mask(b, tiles):
                pool.wait_ge(adj_in, 16 * (b + 1))
                if not early(tiles, 1):
                    pool.wait_ge(masked, tiles)
                if not early(b, 1):
                    pool.wait_ge(mask1_ready, 16 * b)
                settle(pool)
                pool.tensor_scalar(mask_a0[:], adj_t[:], 0.0, MASKED, ALU.is_equal, ALU.mult)\
                    .then_inc(mask0_ready, 1)

            def rstd_of(s, c):
                pool.wait_ge(moments_ready[s], c + 1)
                pool.tensor_tensor(rstd[s][:], var_eps[s][:], minus_half[:], ALU.pow).then_inc(rstd_ready[s], 1)

            def gain_and_shift(s, c, y, norm, dst):
                g = gain[:, norm:norm + 1, :].to_broadcast([P, NT, D])
                h = shift[:, norm:norm + 1, :].to_broadcast([P, NT, D])
                pool.tensor_tensor(dst[:], y[:], g, ALU.mult).then_inc(gained[s], 1)
                pool.wait_ge(gained[s], c + 1)
                pool.tensor_tensor(dst[:], dst[:], h, ALU.add).then_inc(ln_done[s], 1)

            def layer_norm_l0(b, l, dst):
                rstd_of("L", 2 * b + l)
                pool.wait_ge(normed["L"], 2 * b + l + 1)
                gain_and_shift("L", 2 * b + l, y_l, l, dst)

            def residual(b):
                pool.wait_ge(ln_done["L"], 2 * b + 2)
                pool.tensor_tensor(y_f[:], x2[:], bo1[:].unsqueeze(1).to_broadcast([P, NT, D]), ALU.add)\
                    .then_inc(xres_ready, 1)

            def finish(b):
                rstd_of("F", b)
                pool.wait_ge(rstd_ready["F"], b + 1)
                settle(pool)
                for t in range(NT):
                    last = pool.tensor_scalar(y_f[:, t], y_f[:, t], minus_mean["F"][:, t:t + 1],
                                              rstd["F"][:, t:t + 1], ALU.add, ALU.mult)
                last.then_inc(normed["F"], 1)
                pool.wait_ge(normed["F"], b + 1)
                gain_and_shift("F", b, y_f, 2, y_f)
                pool.wait_ge(ln_done["F"], b + 1)
                pool.dma_start(out_v[b], y_f[:]).then_inc(out_stored, 16)
                pool.wait_ge(out_stored, 16 * (b + 1))

            make_mask(0, 0)
            pool.wait_ge(weights_in, 16 * N_WEIGHTS_IN)
            make_mask(1, NT)
            layer_norm_l0(0, 0, x1)
            layer_norm_l0(0, 1, x2)
            layer_norm_l0(1, 0, x1)
            with pool.Fori(0, LOOPS) as i:
                residual(i)
                make_mask(i + 2, (slots_before(i) - 2) * NT)
                layer_norm_l0(i + 1, 1, x2)
                layer_norm_l0(i + 2, 0, x1)
                finish(i)
            residual(NB - 2)
            layer_norm_l0(NB - 1, 1, x2)
            finish(NB - 2)
            residual(NB - 1)
            finish(NB - 1)

        @blk.tensor
        def _(pe):
            def bank(pair, half, before):
                name, b, l = before or (None, None, None)
                if name == "X":
                    pe.wait_ge(xt_ready, 2 * (2 * b + l) + half + 1)
                if name == "QK":
                    pe.wait_ge(qk_ready, 2 * (2 * b + l) + half + 1)
                if name == "AV":
                    pe.wait_ge(ctx_ready, 2 * (2 * b + l) + half + 1)
                if name == "WC":
                    pe.wait_ge(y_ready["L"], 2 * (2 * b + l) + half + 1)
                if name == "X2":
                    pe.wait_ge(xt2_ready, 2 * b + half + 1)
                if name in ("Q", "K"):
                    pe.wait_ge(lo_ready[name], 2 * b + half + 1)
                if name == "V":
                    pe.wait_ge(v_ready, 2 * b + half + 1)
                if name == "OG":
                    pe.wait_ge(rb_ready if half else ot_ready, FIRST + 2 * b + l + 1)
                if name == "WO":
                    pe.wait_ge(y_ready["F"], FIRST + 2 * b + half + 1)
                return ps_j[pair][half]

            def scores(q, r, kind, n, b):
                n_tile = NT * q + r
                if not early(n_tile, 2):
                    pe.wait_ge(masked, n_tile - 1)
                if kind == "L":
                    if r == 0:
                        pe.wait_ge(qk_ready, 2 * (2 * b + n) + 2)
                    for n_, (a, c) in enumerate(PART_PAIRS):
                        last = pe.matmul(ps_s[r % 2][:], qt0[:, a, r * P:(r + 1) * P], kt0[:, c],
                                         start=n_ == 0, stop=n_ == 2)
                    last.then_inc(scores_done, 1)
                else:
                    if r == 0 and n % 4 == 0:
                        pe.wait_ge(stacked[n // 4], 16 * 8 * (b + 1))
                    pe.matmul(ps_s[r % 2][:], stack[:, n, 0, r * P:(r + 1) * P], stack[:, n, 1, :],
                              start=True, stop=True).then_inc(scores_done, 1)

            def split_product(dst, lhs, rhs):
                terms = [(a, c, e) for e in range(DC) for a, c in PART_PAIRS]
                for n, (a, c, e) in enumerate(terms):
                    last = pe.matmul(dst, lhs(a, e), rhs(c, e), start=n == 0, stop=n == len(terms) - 1)
                return last

            def transposes(q, r, kind, n, b):
                pe.wait_ge(exps, NT * q + r + 1)
                if not early(NT * q + r, 2):
                    pe.wait_ge(*(copied(q, r - 2) if r >= 2 else copied(q - 1, r + 2)))
                for t in range(NT):
                    last = pe.transpose(ps_t[r % 2][:, t], probs[:, r, t * P:(t + 1) * P], ident[:])
                last.then_inc(transposed, 1)

            def job(name, pair, b, l, half, before, blk_):
                L = 2 * b + l
                if name == "X":
                    if l == 0:
                        pe.wait_ge(x_in, 16 * (b + 1))
                    else:
                        pe.wait_ge(normed["L"], 2 * b + 1)
                    src = y_l if l else x0
                    out_bank = bank(pair, half, before)
                    for t in range(NT):
                        last = pe.transpose(out_bank[:, t * P:(t + 1) * P], src[:, t, half * P:(half + 1) * P], ident[:])
                    last.then_inc(done["X"], 1)
                if name == "X2":
                    pe.wait_ge(normed["L"], 2 * b + 2)
                    out_bank = bank(pair, half, before)
                    for t in range(NT):
                        last = pe.transpose(out_bank[:, t * P:(t + 1) * P], y_l[:, t, half * P:(half + 1) * P], ident[:])
                    last.then_inc(done["X2"], 1)
                if name == "QK":
                    pe.wait_ge(xt_ready, 2 * L + 2)
                    out_bank = bank(pair, half, before)
                    w = (wq0, wk0)[half]
                    last = split_product(out_bank[:], lambda a, c: w[:, a, l, c], lambda a, c: xt[:, a, c])
                    last.then_inc(done["QK"], 1)
                if name == "AV":
                    r = half
                    pe.wait_ge(*copied(blk_.slot_of("L", l, b), r))
                    src = x1 if l else x0
                    if l == 1 and r == 0:
                        pe.wait_ge(ln_done["L"], 2 * b + 1)
                    for c in range(DC):
                        out_bank = bank(pair, c, before if r == 0 else None)
                        for t in range(NT):
                            last = pe.matmul(out_bank[:, r * P:(r + 1) * P], src[:, t, c * P:(c + 1) * P],
                                             pt_l[:, t, r * P:(r + 1) * P], start=t == 0, stop=t == NT - 1)
                    last.then_inc(done["AV"], 1)
                if name == "WC":
                    pe.wait_ge(ctx_ready, 2 * L + 2)
                    out_bank = bank(pair, half, before)
                    for t in range(2):
                        at = (2 * half + t) * P
                        last = split_product(out_bank[:, t * D:(t + 1) * D],
                                             lambda a, c: ctxt[:, a, c, at:at + P], lambda a, c: wc0[:, a, l, c])
                    last.then_inc(done["WC"], 1)
                if name in "QK" and len(name) == 1:
                    pe.wait_ge(xt2_ready, 2 * b + 2)
                    out_bank = bank(pair, half, before)
                    w = {"Q": wq1, "K": wk1}[name]
                    last = split_product(out_bank[:], lambda a, c: w[:, a, c, half * P:(half + 1) * P],
                                         lambda a, c: xt2[:, a, c])
                    last.then_inc(done[name], 1)
                if name == "V":
                    pe.wait_ge(xt2_ready, 2 * b + 2)
                    out_bank = bank(pair, half, before)
                    for t in range(2):
                        at = (2 * half + t) * P
                        last = split_product(out_bank[:, t * D:(t + 1) * D],
                                             lambda a, c: xt2[:, a, c, at:at + P], lambda a, c: wv1[:, a, c])
                    last.then_inc(done["V"], 1)
                if name == "OG":
                    g, r = l, half
                    if r < NT:
                        pe.wait_ge(*copied(blk_.slot_of("H", 4 * g + 3, b), r))
                        if r == 0:
                            pe.wait_ge(v_ready, 2 * b + 2)
                        out_bank = bank(pair, 0, before if r == 0 else None)
                        for t in range(NT):
                            for h in range(4):
                                col = (4 * g + h) * HD
                                last = pe.matmul(out_bank[h * HD:(h + 1) * HD, r * P:(r + 1) * P],
                                                 v1[:, t, col:col + HD], pt_h[:, h, t, r * P:(r + 1) * P],
                                                 start=t == 0, stop=t == NT - 1)
                        last.then_inc(done["O"], 1)
                    else:
                        pe.wait_ge(r_wide_ready, 2 * b + g + 1)
                        out_bank = bank(pair, 1, before)
                        for t in range(NT):
                            last = pe.transpose(out_bank[:, t * P:(t + 1) * P],
                                                r_wide[:, t].rearrange("p h d -> p (h d)"), ident[:])
                        last.then_inc(done["RB"], 1)
                if name == "WO":
                    pe.wait_ge(ot_ready, FIRST + 2 * b + 2)
                    out_bank = bank(pair, half, before)
                    for t in range(2):
                        at = (2 * half + t) * P
                        for g in range(2):
                            last = pe.matmul(out_bank[:, t * D:(t + 1) * D], ot[:, g, at:at + P], wo1[:, g],
                                             start=g == 0, stop=g == 1)
                    last.then_inc(done["WO"], 1)

            def walk(b_):
                for j in b_.pre:
                    job(*j, b_)
                for k in range(b_.n):
                    ahead = b_.tiles_at(k, AHEAD)
                    if k == 0 and not b_.before:
                        for t in ahead:
                            scores(*t)
                        ahead = []
                    transposes(*b_.tile(k))
                    for t in ahead:
                        scores(*t)
                    for j in b_.jobs.get(k, ()):
                        job(*j, b_)

            def shift_through(n, w, c0, shift_n):
                for c in range(DC):
                    pe.matmul(ps_j[1][1][:, n:n + 1], w(c)[:, c0:c0 + P], shift_c[:, shift_n, c:c + 1],
                              start=c == 0, stop=c == DC - 1)

            pe.sem_inc(done["RB"], FIRST)
            pe.wait_ge(ident_in, 1)
            pe.wait_ge(weights0_in, 16 * N_WEIGHTS0_IN)
            pe.wait_ge(weights_in, 16 * N_WEIGHTS_IN)
            pe.wait_ge(bias_ready, 1)
            for n, name in enumerate(("wq0", "wk0")):
                shift_through(n, lambda c: raw[name][:, (DC + c) * F:(DC + c + 1) * F], 0, 0)
            for n, name in enumerate(("wq1", "wk1")):
                for half in range(DC):
                    shift_through(2 + 2 * n + half, lambda c: raw[name][:, c * D:(c + 1) * D], half * P, 1)
            for c in range(DC):
                last = pe.matmul(ps_j[1][0][:, 0:D], shift_wide[:, c], raw["wv1"][:, c * D:(c + 1) * D],
                                 start=c == 0, stop=c == DC - 1)
            last.then_inc(bias_sums, 1)
            pe.wait_ge(bias_ready, 2)
            pe.wait_ge(weights_ready, 1)
            program(walk, pe.Fori)

        @blk.scalar
        def _(act):
            def exp(q, r, kind, n, b):
                tile = NT * q + r
                act.wait_ge(masked, tile + 1)
                if not early(tile, 4):
                    act.wait_ge(transposed, tile - 3)
                nm, total = (nm_l, sum_l) if kind == "L" else (nm_h, sum_h)
                act.activation(probs[:, r], masked_s[:, r], ACT.Exp, bias=nm[:, n, r:r + 1], scale=-1.0,
                               accum_out=total[:, n, r:r + 1]).then_inc(exps, 1)

            def copy_tile(q, r, kind, n, b):
                act.wait_ge(transposed, NT * q + r + 1)
                dst = (pt_l if kind == "L" else pt_h[:, n % 4])[:, :, r * P:(r + 1) * P]
                act.activation(dst, ps_t[r % 2][:], ACT.Copy).then_inc(copied_act, 1)

            def job(name, pair, b, l, half, before, blk_):
                L = 2 * b + l
                if pair is None:
                    return
                bank = ps_j[pair][half % 2][:]
                if name == "X":
                    act.wait_ge(done["X"], 2 * L + half + 1)
                    act.activation(xt[:, 0, half], bank, ACT.Copy).then_inc(xt_hi, 1)
                if name == "X2":
                    act.wait_ge(done["X2"], 2 * b + half + 1)
                    act.activation(xt2[:, 0, half], bank, ACT.Copy).then_inc(xt2_hi, 1)
                if name == "QK":
                    act.wait_ge(done["QK"], 2 * L + half + 1)
                    dst, bias = ((qt0, bq0), (kt0, bk0))[half]
                    act.activation(dst[:, 0], bank, ACT.Identity, bias=bias[:, l:l + 1]).then_inc(qk_hi, 1)
                if name == "AV":
                    if half == NT - 1:
                        act.wait_ge(done["AV"], NT * (L + 1))
                        for c in range(DC):
                            act.activation(ctxt[:, 0, c], ps_j[pair][c][:], ACT.Copy).then_inc(ctx_hi, 1)
                if name in "QK" and len(name) == 1:
                    act.wait_ge(done[name], DC * b + half + 1)
                    if not early(b, 1):
                        act.wait_ge(bounced[half], 16 * b)
                    a, bias = {"Q": (0, bq1), "K": (2, bk1)}[name]
                    act.activation(parts[:, half, a], bank, ACT.Identity, bias=bias[:, half:half + 1])\
                        .then_inc(hi_ready[name], 1)
                if name == "OG" and half == NT:
                    g = l
                    act.wait_ge(done["RB"], FIRST + 2 * b + g + 1)
                    act.wait_ge(ot_ready, FIRST + 2 * b + g)
                    act.activation(rb[:], ps_j[pair][1][:], ACT.Copy).then_inc(rb_ready, 1)

            def walk(b_):
                for j in b_.pre:
                    job(*j, b_)
                for k in range(b_.n):
                    for t in b_.tiles_at(k, 1):
                        exp(*t)
                    copy_now(b_, k)
                    for j in b_.late_jobs(k):
                        job(*j, b_)

            def copy_now(b_, k):
                t = b_.tile(k)
                if t[1] != DVE_TILE:
                    copy_tile(*t)

            act.sem_inc(rb_ready, FIRST)
            act.wait_ge(scaled, 1)
            for n, (name, w) in enumerate(split_weights):
                act.activation(w(0), raw[name], ACT.Copy).then_inc(weights_hi, 1)
            act.wait_ge(weights_ready, 1)
            program(walk, act.Fori)

        @blk.vector
        def _(dve):
            def mask(q, r, kind, n, b):
                tile = NT * q + r
                dve.wait_ge(scores_done, tile + 1)
                if not early(tile, 4):
                    dve.wait_ge(exps, tile - 3)
                if kind == "L":
                    if r == 0:
                        dve.wait_ge(*((mask1_ready, 16 * (b + 1)) if n else (mask0_ready, b + 1)))
                    m, nm, scale = (mask_a0, mask_a1)[n], nm_l, L0_SCALE
                else:
                    if n == 0:
                        dve.wait_ge(maskh_ready[r], 16 * (b + 1))
                    m, nm, scale = mask_h, nm_h, L1_SCALE
                settle(dve)
                dve.tensor_tensor_reduce(out=masked_s[:, r], in0=ps_s[r % 2][:], in1=m[:, r], scale=-scale,
                                         scalar=BIG, op0=ALU.add, op1=ALU.min,
                                         accum_out=nm[:, n, r:r + 1]).then_inc(masked, 1)

            def copy_tile(q, r, kind, n, b):
                dve.wait_ge(transposed, NT * q + r + 1)
                dst = (pt_l if kind == "L" else pt_h[:, n % 4])[:, :, r * P:(r + 1) * P]
                dve.tensor_copy(dst, ps_t[r % 2][:]).then_inc(copied_dve, 1)

            def statistics(s, c, y, half):
                dve.wait_ge(y_ready[s], (FIRST if s == "F" else 0) + 2 * c + half + 1)
                for t in range(2 * half, 2 * half + 2):
                    last = dve.bn_stats(stats[s][:, t], y[:, t])
                last.then_inc(stats_ready[s], 1)
                if half == 1:
                    dve.wait_ge(stats_ready[s], 2 * c + 2)
                    settle(dve)
                    for t in range(NT):
                        last = dve.bn_aggr(moments[s][:, t], stats[s][:, t])
                    last.then_inc(aggregated[s], 1)
                    dve.wait_ge(aggregated[s], c + 1)
                    dve.tensor_scalar(minus_mean[s][:], moments[s][:, :, 0], -1.0, None, ALU.mult)
                    dve.tensor_scalar(var_eps[s][:], moments[s][:, :, 1], LN_EPS, None, ALU.add)\
                        .then_inc(moments_ready[s], 1)

            def low_part(dst, full, high, ready):
                dve.tensor_tensor(dst, full, high, ALU.subtract).then_inc(ready, 1)

            def job(name, pair, b, l, half, before, blk_):
                L = 2 * b + l
                if name == "N":
                    dve.wait_ge(rstd_ready["L"], L + 1)
                    for t in range(NT):
                        last = dve.tensor_scalar(y_l[:, t], y_l[:, t], minus_mean["L"][:, t:t + 1],
                                                 rstd["L"][:, t:t + 1], ALU.add, ALU.mult)
                    last.then_inc(normed["L"], 1)
                    return
                if name == "R":
                    g = l
                    G = 2 * b + g
                    dve.wait_ge(exps, NT * (blk_.slot_of("H", 4 * g + 3, b) + 1))
                    heads = slice(4 * g, 4 * g + 4)
                    dve.scalar_tensor_tensor(sum_f[:], nm_h[:, heads], ALL_MASKED, sum_h[:, heads],
                                             ALU.is_lt, ALU.mult).then_inc(sum_f_ready, 1)
                    dve.wait_ge(sum_f_ready, G + 1)
                    dve.reciprocal(r_h[:], sum_f[:]).then_inc(r_h_ready, 1)
                    dve.wait_ge(r_h_ready, G + 1)
                    dve.wait_ge(done["RB"], FIRST + G)
                    dve.tensor_copy(r_wide[:].rearrange("p t h d -> p h t d"),
                                    r_h[:].unsqueeze(3).to_broadcast([P, 4, NT, HD]))\
                        .then_inc(r_wide_ready, 1)
                    return
                bank = ps_j[pair][half % 2][:]
                two = bank.rearrange("p (t d) -> p t d", t=2)
                nts = slice(2 * half, 2 * half + 2)
                if name == "X":
                    dve.wait_ge(xt_hi, 2 * L + half + 1)
                    low_part(xt[:, 1, half], bank, xt[:, 0, half].bitcast(fp32), xt_ready)
                if name == "X2":
                    dve.wait_ge(xt2_hi, 2 * b + half + 1)
                    low_part(xt2[:, 1, half], bank, xt2[:, 0, half].bitcast(fp32), xt2_ready)
                if name == "AV":
                    if half == NT - 1:
                        for c in range(DC):
                            dve.wait_ge(ctx_hi, 2 * L + c + 1)
                            low_part(ctxt[:, 1, c], ps_j[pair][c][:], ctxt[:, 0, c].bitcast(fp32), ctx_ready)
                if name == "QK":
                    dve.wait_ge(qk_hi, 2 * L + half + 1)
                    dst, bias = ((qt0, bq0), (kt0, bk0))[half]
                    dve.scalar_tensor_tensor(dst[:, 1], bank, bias[:, l:l + 1], dst[:, 0].bitcast(fp32),
                                             ALU.add, ALU.subtract).then_inc(qk_ready, 1)
                if name == "WC":
                    if half == 0:
                        dve.wait_ge(done["WC"], 2 * L + 1)
                        dve.reciprocal(rinv_l[:], sum_l[:, l]).then_inc(rinv_ready, 1)
                        dve.wait_ge(rinv_ready, L + 1)
                        dve.scalar_tensor_tensor(r_l[:], nm_l[:, l], ALL_MASKED, rinv_l[:], ALU.is_lt,
                                                 ALU.mult).then_inc(r_l_ready, 1)
                        dve.wait_ge(r_l_ready, L + 1)
                    dve.wait_ge(done["WC"], 2 * L + half + 1)
                    if not early(L, 1):
                        dve.wait_ge(ln_done["L"], L)
                    if l == 0:
                        dve.wait_ge(x_in, 16 * (b + 1))
                    src = x1 if l else x0
                    for t in range(2):
                        nt = 2 * half + t
                        last = dve.scalar_tensor_tensor(y_l[:, nt], two[:, t], r_l[:, nt:nt + 1], src[:, nt],
                                                        ALU.mult, ALU.add)
                    last.then_inc(y_ready["L"], 1)
                    statistics("L", L, y_l, half)
                if name in "QK" and len(name) == 1:
                    dve.wait_ge(hi_ready[name], DC * b + half + 1)
                    a, bias = {"Q": (0, bq1), "K": (2, bk1)}[name]
                    dve.scalar_tensor_tensor(parts[:, half, a + 1], bank, bias[:, half:half + 1],
                                             parts[:, half, a], ALU.add, ALU.subtract)\
                        .then_inc(lo_ready[name], 1)
                if name == "V":
                    dve.wait_ge(done["V"], 2 * b + half + 1)
                    dve.tensor_tensor(v1[:, nts], two, bv1[:].unsqueeze(1).to_broadcast([P, 2, D]), ALU.add)\
                        .then_inc(v_ready, 1)
                if name == "OG" and half == NT:
                    g = l
                    dve.wait_ge(done["O"], NT * (2 * b + g + 1))
                    dve.wait_ge(rb_ready, FIRST + 2 * b + g + 1)
                    dve.tensor_tensor(ot[:, g], ps_j[pair][0][:], rb[:], ALU.mult).then_inc(ot_ready, 1)
                if name == "WO":
                    dve.wait_ge(done["WO"], 2 * b + half + 1)
                    dve.wait_ge(xres_ready, b + 1)
                    dve.tensor_tensor(y_f[:, nts], two, y_f[:, nts], ALU.add).then_inc(y_ready["F"], 1)
                    statistics("F", b, y_f, half)

            def walk(b_):
                for j in b_.pre:
                    job(*j, b_)
                for k in range(b_.n):
                    for t in b_.tiles_at(k, 2):
                        mask(*t)
                    t = b_.tile(k)
                    if t[1] == DVE_TILE:
                        copy_tile(*t)
                    for j in b_.late_jobs(k):
                        job(*j, b_)

            dve.sem_inc(y_ready["F"], FIRST)
            dve.sem_inc(ot_ready, FIRST)
            dve.wait_ge(weights0_in, 16 * N_WEIGHTS0_IN)
            dve.wait_ge(weights_in, 16 * N_WEIGHTS_IN)
            dve.tensor_copy(shift_wide[:], shift_c[:, 1].unsqueeze(2).to_broadcast([P, DC, P]))\
                .then_inc(bias_ready, 1)
            dve.wait_ge(bias_sums, 1)
            sums = ps_j[1][1]
            dve.tensor_tensor(bq0[:, 1:2], bq0[:, 1:2], sums[:, 0:1], ALU.add)
            dve.tensor_tensor(bk0[:, 1:2], bk0[:, 1:2], sums[:, 1:2], ALU.add)
            dve.tensor_tensor(bq1[:], bq1[:], sums[:, 2:4], ALU.add)
            dve.tensor_tensor(bk1[:], bk1[:], sums[:, 4:6], ALU.add)
            dve.tensor_tensor(bv1[:], bv1[:], ps_j[1][0][:, 0:D], ALU.add).then_inc(bias_ready, 1)
            for c in range(DC):
                for name in ("wq0", "wk0"):
                    w = raw[name][:, (DC + c) * F:(DC + c + 1) * F]
                    dve.tensor_scalar(w, w, gain_c[:, 0, c:c + 1], None, ALU.mult)
                for name in ("wq1", "wk1", "wv1"):
                    w = raw[name][:, c * D:(c + 1) * D]
                    last = dve.tensor_scalar(w, w, gain_c[:, 1, c:c + 1], None, ALU.mult)
            last.then_inc(scaled, 1)
            for n, (name, w) in enumerate(split_weights):
                dve.wait_ge(weights_hi, n + 1)
                last = dve.tensor_tensor(w(1), raw[name], w(0).bitcast(fp32), ALU.subtract)
            last.then_inc(weights_ready, 1)
            program(walk, dve.Fori)


def kernel(**inputs):
    import numpy as _np
    import concourse.bacc as _bacc
    from concourse import mybir as _mybir
    from concourse.bass_utils import run_bass_kernel_spmd as _run

    nc = _bacc.Bacc("TRN2", target_bir_lowering=False, num_devices=1)
    arrays = {}

    def dram(name, a):
        a = _np.ascontiguousarray(a)
        arrays[name] = a
        return nc.dram_tensor(name, a.shape, _mybir.dt.from_np(a.dtype), kind="ExternalInput").ap()

    def arr(name):
        return _np.asarray(inputs[name])

    x = dram("x_dram", arr("x"))
    adj = dram("adj_dram", arr("adj"))
    l0 = {
        "Wq": dram("l0_wq", arr("L0_gnn_Wq").transpose(0, 2, 1)),
        "Wk": dram("l0_wk", arr("L0_gnn_Wk").transpose(0, 2, 1)),
        "Wc": dram("l0_wc", arr("L0_gnn_Wc").transpose(0, 2, 1)),
        "bq": dram("l0_bq", arr("L0_gnn_bq").T),
        "bk": dram("l0_bk", arr("L0_gnn_bk").T),
        "g": dram("l0_g", arr("L0_gnn_ln_g")),
        "g_c": dram("l0_g_columns", arr("L0_gnn_ln_g").reshape(2 * DC, P).T),
        "b_c": dram("l0_b_columns", arr("L0_gnn_ln_b").reshape(2 * DC, P).T),
        "b": dram("l0_b", arr("L0_gnn_ln_b")),
    }
    l1 = {
        "Wq": dram("l1_wq", arr("L1_gnn_Wq")),
        "Wk": dram("l1_wk", arr("L1_gnn_Wk")),
        "Wv": dram("l1_wv", arr("L1_gnn_Wv")),
        "Wo": dram("l1_wo", arr("L1_gnn_Wo")),
        "bq": dram("l1_bq", arr("L1_gnn_bq").reshape(2, 128).T),
        "bk": dram("l1_bk", arr("L1_gnn_bk").reshape(2, 128).T),
        "bv": dram("l1_bv", arr("L1_gnn_bv")),
        "bo": dram("l1_bo", arr("L1_gnn_bo")),
        "g": dram("l1_g", arr("L1_gnn_gamma")),
        "b": dram("l1_b", arr("L1_gnn_beta")),
    }
    out = nc.dram_tensor("out_dram", arrays["x_dram"].shape, _mybir.dt.float32, kind="ExternalOutput").ap()
    graph_attention(nc, x, adj, l0, l1, out)
    r = _run(nc, [arrays], core_ids=[0])
    return r.results[0]["out_dram"]
```

```python
from contextlib import ExitStack

import concourse.bass as bass
from concourse import mybir

P = 128
NB, N, D = 16, 512, 256
F = 128
H, HD = 8, 32
NT = N // P
DC = D // P
LN_EPS = 1e-5
L0_SCALE = float(F) ** -0.5
L1_SCALE = float(HD) ** -0.5
MASKED = -1e30
ALL_MASKED = 1e28
BIG = 3e38

LOOP_SLOTS = [("H", 2, "i"), ("L", 1, "i+1"), ("H", 3, "i"), ("H", 4, "i"), ("H", 5, "i"), ("L", 0, "i+2"),
              ("H", 6, "i"), ("H", 7, "i"), ("H", 0, "i+1"), ("H", 1, "i+1")]
LOOPS = NB - 2
TAIL_SLOTS = ([("H", 2, "i"), ("L", 1, "i+1")] + [("H", h, "i") for h in range(3, 8)]
              + [("H", h, "i+1") for h in range(8)])
AHEAD = 3

LOOP_JOBS = [
    ("V", 1, "i", 0, (0, 1)),
    ("X", 0, "i+2", 0, (0, 2)),
    ("M", None, "i+2", 0, (3,)),
    ("QK", 1, "i+2", 0, (4, 5)),
    ("AV", 1, "i+1", 1, (6, 7, 8, 9)),
    ("OG", 1, "i", 0, (11, 13, 16)),
    ("N", None, "i+1", 1, (11,)),
    ("M", None, "i+2", 1, (11,)),
    ("R", None, "i", 0, (13,)),
    ("X2", 0, "i+1", 0, (14, 15)),
    ("XW", 0, "i+2", 0, (16, 18)),
    ("QH", 0, "i+1", 0, (20, 21)),
    ("AV", 0, "i+2", 0, (22, 24, 24, 25)),
    ("QH", 0, "i+1", 1, (26, 28)),
    ("N", None, "i+2", 0, (27,)),
    ("X", 1, "i+2", 1, (29, 29)),
    ("R", None, "i", 1, (31,)),
    ("OG", 0, "i", 1, (31, 33, 34)),
    ("QK", 1, "i+2", 1, (32, 32)),
    ("XW", 1, "i+2", 1, (35, 39)),
    ("WO", 0, "i", 0, (37, 37)),
]
PRO_BLOCKS = [
    ([("L", 0, 0)], [("X", 0, 0, 0), ("S", 1, 0, 0), ("QK", 0, 0, 0)],
     [("XW", 1, 0, 0, (0, 0)), ("W", None, 0, 1, (1,)), ("AV", 0, 0, 0, (2, 3, 3, 3)), ("N", None, 0, 0, (3,))]),
    ([("L", 1, 0)], [("X", 1, 0, 1), ("QK", 0, 0, 1)],
     [("M", None, 1, 0, (0,)), ("XW", 1, 0, 1, (0, 0)), ("W", None, 0, 2, (1,)), ("AV", 0, 0, 1, (2, 3, 3, 3)), ("X", 1, 1, 0, (3, 3)), ("N", None, 0, 1, (3,)), ("M", None, 1, 1, (3,)),
      ("X2", 0, 0, 0, (3, 3)), ("QK", 1, 1, 0, (3, 3)), ("QH", 0, 0, 0, (3, 3)), ("XW", 1, 1, 0, (3, 3)),
      ("QH", 0, 0, 1, (3, 3))]),
    ([("L", 0, 1), ("H", 0, 0), ("H", 1, 0)], [],
     [("AV", 1, 1, 0, (2, 3, 4, 4)), ("N", None, 1, 0, (5,)),
      ("X", 1, 1, 1, (7, 7)), ("QK", 0, 1, 1, (9, 9)), ("XW", 1, 1, 1, (10, 11))]),
]
TAIL_JOBS = [
    ("V", 0, "i", 0, (0, 0)),
    ("AV", 1, "i+1", 1, (6, 8, 8, 9)),
    ("R", None, "i", 0, (10,)),
    ("N", None, "i+1", 1, (11,)),
    ("OG", 1, "i", 0, (11, 12, 14)),
    ("X2", 0, "i+1", 0, (13, 13)),
    ("QH", 0, "i+1", 0, (15, 16)),
    ("QH", 1, "i+1", 1, (18, 19)),
    ("OG", 1, "i", 1, (26, 28, 29)),
    ("R", None, "i", 1, (26,)),
    ("V", 0, "i+1", 0, (30, 31)),
    ("WO", 0, "i", 0, (33, 35)),
    ("R", None, "i+1", 0, (42,)),
    ("OG", 0, "i+1", 0, (43, 45, 48)),
    ("R", None, "i+1", 1, (59,)),
    ("OG", 0, "i+1", 1, (59, 59, 59)),
    ("WO", 1, "i+1", 0, (59, 59)),
]
PARTS = {"AV": 4, "OG": 3, "R": 1, "N": 1, "S": 1, "W": 1, "M": 1}
DVE_TILES, LAST_DVE_TILES = (3,), (1, 3)


def graph_attention(nc, x, adj, l0, l1, out):
    fp32, fp16, bf16, i32 = mybir.dt.float32, mybir.dt.float16, mybir.dt.bfloat16, mybir.dt.int32
    fp32r = mybir.dt.float32r
    ALU, ACT = mybir.AluOpType, mybir.ActivationFunctionType

    x_v = x.rearrange("b (t p) d -> b p t d", p=P)
    adj_v = adj.rearrange("b (t p) k -> b p t k", p=P)
    out_v = out.rearrange("b (t p) d -> b p t d", p=P)

    ctx = ExitStack()
    with ctx:
        def sb(name, shape, dt=fp32):
            return ctx.enter_context(nc.sbuf_tensor(name, shape, dt))

        def sem(name):
            return ctx.enter_context(nc.semaphore(name))

        wq0 = sb("wq0", [P, 2, 2, DC, F], fp32r)
        wk0 = sb("wk0", [P, 2, 2, DC, F], fp32r)
        wc0 = sb("wc0", [P, 2, 2, DC, D], fp32r)
        wq1 = sb("wq1", [P, 2, DC, D], fp32r)
        wk1 = sb("wk1", [P, 2, DC, D], fp32r)
        wv1 = sb("wv1", [P, 2, DC, D], fp32r)
        wo1 = sb("wo1", [P, DC, D])
        bq0 = sb("bq0", [P, 2])
        bk0 = sb("bk0", [P, 2])
        bq1 = sb("bq1", [P, DC])
        bk1 = sb("bk1", [P, DC])
        gain_c = sb("gain_c", [P, 2, DC])
        shift_c = sb("shift_c", [P, 2, DC])
        bx1 = sb("bx1", [P, D], fp32r)
        mean_64 = sb("mean_64", [P, P], fp32r)
        bv1 = sb("bv1", [P, D])
        gain = sb("gain", [P, 3, D])
        shift = sb("shift", [P, 3, D])
        ident = sb("ident", [P, P])
        minus_half = sb("minus_half", [P, NT])
        x0 = sb("x0", [P, NT, D])
        x1 = sb("x1", [P, NT, D])
        x2 = sb("x2", [P, NT, D])
        adj_t = sb("adj_t", [P, NT // 2, N], i32)
        mask_a0 = sb("mask_a0", [P, NT, N], bf16)
        mask_a1 = sb("mask_a1", [P, NT, N], bf16)
        mask_h = sb("mask_h", [P, NT, N], bf16)
        xt = sb("xt", [P, 2, DC, N], fp32r)
        qt0 = sb("qt0", [P, 2, N], fp32r)
        kt0 = sb("kt0", [P, 2, N], fp32r)
        xw = sb("xw", [P, 2, NT, D], fp32r)
        pt_l = sb("pt_l", [P, 2, NT, N], fp32r)
        y_l = sb("y_l", [P, NT, D])
        xt2 = sb("xt2", [P, 2, DC, N], fp32r)
        parts = sb("parts", [P, DC, 4, N], fp16)
        stack = sb("stack", [P, H, 2, N], fp16)
        v1 = sb("v1", [P, NT, D])
        pt_h = sb("pt_h", [P, 4, NT, N])
        rb = sb("rb", [P, N])
        ot = sb("ot", [P, 2, N])
        y_f = sb("y_f", [P, NT, D])
        masked_s = sb("masked_s", [P, 4, N])
        probs = sb("probs", [P, 4, N])
        nm_l = sb("nm_l", [P, 2, NT])
        nm_h = sb("nm_h", [P, H, NT])
        sum_l = sb("sum_l", [P, 2, NT])
        sum_h = sb("sum_h", [P, H, NT])
        rinv_l = sb("rinv_l", [P, NT])
        r_l = sb("r_l", [P, NT])
        sum_f = sb("sum_f", [P, 4, NT])
        r_h = sb("r_h", [P, 4, NT])
        r_wide = ot[:, 1].rearrange("p (t h d) -> p t h d", t=NT, h=4)
        stats = {s: sb(f"stats_{s}", [P, NT, 6]) for s in "LF"}
        moments = {s: sb(f"moments_{s}", [P, NT, 2]) for s in "LF"}
        minus_mean = {s: sb(f"minus_mean_{s}", [P, NT]) for s in "LF"}
        var_eps = {s: sb(f"var_eps_{s}", [P, NT]) for s in "LF"}
        rstd = {s: sb(f"rstd_{s}", [P, NT]) for s in "LF"}

        shift_wide = rb[:].rearrange("p (l c n) -> p l c n", l=2, c=DC)
        bo1 = ot[:, 1, 0:D]

        adj_spare = mask_h[:].rearrange("p t n -> p (t n)").bitcast(i32).rearrange("p (t n) -> p t n", t=2)

        raw_flat = pt_h[:].rearrange("p h t n -> p (h t n)")
        raw, at = {}, 0
        for name, width in (("wq0", 2 * DC * F), ("wk0", 2 * DC * F), ("wc0", 2 * DC * D),
                            ("wq1", DC * D), ("wk1", DC * D), ("wv1", DC * D)):
            raw[name] = raw_flat[:, at:at + width]
            at += width

        ps_s = [ctx.enter_context(nc.psum_tensor(f"ps_s{n}", [P, N], fp32)) for n in range(2)]
        ps_t = [ctx.enter_context(nc.psum_tensor(f"ps_t{n}", [P, NT, P], fp32)) for n in range(2)]
        ps_j = [[ctx.enter_context(nc.psum_tensor(f"ps_j{a}{h}", [P, N], fp32)) for h in range(2)]
                for a in range(2)]
        bounce = nc.dram_tensor("bounce", [DC, 4, HD, 4, N], fp16).ap()

        weights_in = sem("weights_in")
        ident_zero, ident_in, half_in = sem("ident_zero"), sem("ident_in"), sem("half_in")
        mean_in, bo_added, bx1_hi = sem("mean_in"), sem("bo_added"), sem("bx1_hi")
        pt_lo_ready, xw_hi = sem("pt_lo_ready"), sem("xw_hi")
        x_in, adj_in = sem("x_in"), sem("adj_in")
        mask0_ready, mask1_ready = sem("mask0_ready"), sem("mask1_ready")
        maskh_ready = [sem(f"maskh{r}_ready") for r in range(NT)]
        scores_done, masked, exps = sem("scores_done"), sem("masked"), sem("exps")
        transposed, copied_act, copied_dve = sem("transposed"), sem("copied_act"), sem("copied_dve")
        done = {j: sem(f"{j}_done") for j in
                ("X", "QK", "AV", "XW", "X2", "Q", "K", "V", "O", "RB", "WO")}
        xt_hi, qk_hi, xt2_hi = sem("xt_hi"), sem("qk_hi"), sem("xt2_hi")
        xt_ready, qk_ready, xw_ready = sem("xt_ready"), sem("qk_ready"), sem("xw_ready")
        xt2_ready, v_ready = sem("xt2_ready"), sem("v_ready")
        weights0_in, biases_in, wide_ready = sem("weights0_in"), sem("biases_in"), sem("wide_ready")
        bias_sums, bias_ready = sem("bias_sums"), sem("bias_ready")
        scaled, weights_hi, weights_ready = sem("scaled"), sem("weights_hi"), sem("weights_ready")
        hi_ready = {j: sem(f"{j}_hi_ready") for j in "QK"}
        lo_ready = {j: sem(f"{j}_lo_ready") for j in "QK"}
        bounced = [sem(f"bounced{c}") for c in range(DC)]
        stacked = [sem(f"stacked{c}") for c in range(DC)]
        rinv_ready, r_l_ready = sem("rinv_ready"), sem("r_l_ready")
        sum_f_ready, r_h_ready, r_wide_ready = sem("sum_f_ready"), sem("r_h_ready"), sem("r_wide_ready")
        rb_ready, ot_ready = sem("rb_ready"), sem("ot_ready")
        y_ready = {s: sem(f"y_ready_{s}") for s in "LF"}
        stats_ready = {s: sem(f"stats_ready_{s}") for s in "LF"}
        aggregated = {s: sem(f"aggregated_{s}") for s in "LF"}
        moments_ready = {s: sem(f"moments_ready_{s}") for s in "LF"}
        rstd_ready = {s: sem(f"rstd_ready_{s}") for s in "LF"}
        normed = {s: sem(f"normed_{s}") for s in "LF"}
        gained = {s: sem(f"gained_{s}") for s in "LF"}
        ln_done = {s: sem(f"ln_done_{s}") for s in "LF"}
        xres_ready, out_stored = sem("xres_ready"), sem("out_stored")
        last_rows, last_stored = sem("last_rows"), sem("last_stored")

        waits_passed = sem("waits_passed")


        FIRST = 2

        N_WEIGHTS0_IN = 2 + 3 + 3
        N_BIASES_IN = 5
        N_WEIGHTS_IN = 2 + 2 * 3

        def slots_before(i):
            return sum(len(slots) for slots, _, _ in PRO_BLOCKS) + len(LOOP_SLOTS) * i

        LAST_SLOTS = slots_before(LOOPS) + len(TAIL_SLOTS) - H

        def by_dve(q, r):
            return r in (LAST_DVE_TILES if isinstance(q, int) and q >= LAST_SLOTS else DVE_TILES)

        def copied(q, r):
            mine = [t for t in range(NT) if by_dve(q, t) == by_dve(q, r)]
            before = q * (len(DVE_TILES) if by_dve(q, r) else NT - len(DVE_TILES))
            if isinstance(q, int) and q >= LAST_SLOTS:
                more = (q - LAST_SLOTS) * (len(LAST_DVE_TILES) - len(DVE_TILES))
                before += more if by_dve(q, r) else -more
            return copied_dve if by_dve(q, r) else copied_act, before + mine.index(r) + 1

        def early(count, n):
            return isinstance(count, int) and count < n

        def settle(eng):
            eng.sem_inc(waits_passed, 1)

        def program(walk, loop):
            q, last = 0, []
            for n, (slots, pre, jobs) in enumerate(PRO_BLOCKS):
                after = ("H", 2, 0) if n == len(PRO_BLOCKS) - 1 else None
                walk(block(q, slots, pre=pre, jobs=jobs, last=last, after=after))
                q += len(slots)
                last += [row[:4] for row in (*pre, *jobs)]

            def named(rows, i):
                graph_of = {"i": i, "i+1": i + 1, "i+2": i + 2}
                return [tuple(graph_of.get(v, v) if isinstance(v, str) else v for v in row) for row in rows]

            def before_loop_body(i):
                return [("WO", 0, i - 1, 0), ("XW", 1, i + 1, 1)]

            with loop(0, LOOPS) as i:
                walk(block(slots_before(i), named(LOOP_SLOTS, i), jobs=named(LOOP_JOBS, i),
                           last=before_loop_body(i), before=True, after=("H", 2, i + 1)))
            i = LOOPS
            walk(block(slots_before(i), named(TAIL_SLOTS, i), jobs=named(TAIL_JOBS, i),
                       last=before_loop_body(i), before=True))

        class block:

            def __init__(self, q0, slots, pre=(), jobs=(), last=(), before=False, after=None):
                self.q0, self.slots, self.before, self.after = q0, slots, before, after
                self.n = len(slots) * NT
                in_bank = {pair: (name, b, l) for name, pair, b, l in last if pair is not None}
                self.pre, self.jobs = [], {}
                for name, pair, b, l in pre:
                    halves = range(PARTS.get(name, 2))
                    self.pre += [(name, pair, b, l, half, in_bank.get(pair)) for half in halves]
                    in_bank[pair] = (name, b, l)
                for name, pair, b, l, steps in jobs:
                    for half, k in enumerate(steps):
                        self.jobs.setdefault(k, []).append((name, pair, b, l, half, in_bank.get(pair)))
                    in_bank[pair] = (name, b, l)

            def tile(self, k):
                s, r = k // NT, k % NT
                if s < len(self.slots):
                    return (self.q0 + s, r, *self.slots[s])
                return None if self.after is None else (self.q0 + s, r, *self.after)

            def tiles_at(self, k, ahead):
                first = not self.before and k == 0
                ks = range(0 if first else k + ahead, k + ahead + 1)
                return [t for t in map(self.tile, ks) if t is not None]

            def slot_of(self, kind, n, b):
                for s, (kind_, n_, b_) in enumerate(self.slots):
                    same_graph = b is b_ or (isinstance(b, int) and isinstance(b_, int) and b == b_)
                    if (kind_, n_) == (kind, n) and same_graph:
                        return self.q0 + s
                return self.q0 - 1

            def late_jobs(self, k):
                got = list(self.jobs.get(k - 1, ()))
                return got + (list(self.jobs.get(k, ())) if k >= self.n - 1 else [])

        PART_PAIRS = ((0, 0), (0, 1), (1, 0))
        split_weights = [
            [(raw["wq0"][:, l * DC * F:(l + 1) * DC * F], lambda a, l=l: wq0[:, a, l].rearrange("p c f -> p (c f)")),
             (raw["wk0"][:, l * DC * F:(l + 1) * DC * F], lambda a, l=l: wk0[:, a, l].rearrange("p c f -> p (c f)")),
             (raw["wc0"][:, l * DC * D:(l + 1) * DC * D], lambda a, l=l: wc0[:, a, l].rearrange("p c f -> p (c f)"))]
            for l in range(2)]
        split_weights += [[
            (raw["wq1"], lambda a: wq1[:, a].rearrange("p c f -> p (c f)")),
            (raw["wk1"], lambda a: wk1[:, a].rearrange("p c f -> p (c f)")),
            (raw["wv1"], lambda a: wv1[:, a].rearrange("p c f -> p (c f)")),
        ]]

        blk = ctx.enter_context(nc.Block())

        @blk.sync
        def _(sp):
            def load_adj(b, h):
                if not early(b, 1):
                    sp.wait_ge(mask0_ready, 2 * b + h)
                    settle(sp)
                dst = adj_spare if early(b, 1) and h == 1 else adj_t[:]
                sp.dma_start(dst, adj_v[b][:, 2 * h:2 * h + 2]).then_inc(adj_in, 16)

            sp.dma_start(x0[:], x_v[0]).then_inc(x_in, 16)
            for dst, src in ((gain_c[:].rearrange("p l c -> p (l c)"), l0["g_c"]),
                             (shift_c[:].rearrange("p l c -> p (l c)"), l0["b_c"])):
                sp.dma_start(dst, src).then_inc(weights0_in, 16)
            for name, src in (("wq0", l0["Wq"]), ("wk0", l0["Wk"]), ("wc0", l0["Wc"])):
                sp.dma_start(raw[name].rearrange("p (l c f) -> p l c f", l=2, c=DC),
                             src.rearrange("l (c p) f -> p l c f", p=P)).then_inc(weights0_in, 16)
            for name, src in (("wq1", l1["Wq"]), ("wk1", l1["Wk"]), ("wv1", l1["Wv"])):
                sp.dma_start(raw[name].rearrange("p (c e) -> p c e", c=DC),
                             src.rearrange("(c p) e -> p c e", p=P)).then_inc(weights0_in, 16)
            for dst, src in ((bq0, l0["bq"]), (bk0, l0["bk"]), (bq1, l1["bq"]), (bk1, l1["bk"])):
                sp.dma_start(dst[:], src).then_inc(biases_in, 16)
            load_adj(0, 0)
            load_adj(0, 1)
            sp.dma_start(bv1[:], l1["bv"].partition_broadcast(P)).then_inc(biases_in, 16)
            sp.dma_start(wo1[:], l1["Wo"].rearrange("(c p) e -> p c e", p=P)).then_inc(weights_in, 16)
            sp.dma_start(bo1, l1["bo"].partition_broadcast(P)).then_inc(weights_in, 16)
            for n, (g, s) in enumerate(((l0["g"][0], l0["b"][0]), (l0["g"][1], l0["b"][1]), (l1["g"], l1["b"]))):
                sp.dma_start(gain[:, n], g.partition_broadcast(P)).then_inc(weights_in, 16)
                sp.dma_start(shift[:, n], s.partition_broadcast(P)).then_inc(weights_in, 16)

            def load_x(b):
                sp.wait_ge(y_ready["L"], 2 * (2 * (b - 1) + 1))
                settle(sp)
                sp.dma_start(x0[:], x_v[b]).then_inc(x_in, 16)

            def copy_mask1(b):
                if not early(b, 1):
                    for r in range(NT):
                        sp.wait_ge(maskh_ready[r], 16 * b)
                        settle(sp)
                sp.wait_ge(mask0_ready, 2 * (b + 1))
                settle(sp)
                sp.dma_start(mask_a1[:], mask_a0[:]).then_inc(mask1_ready, 16)

            def copy_maskh(b, tiles, each):
                for r in range(NT):
                    sp.wait_ge(masked, tiles + each * (r + 1))
                    settle(sp)
                    sp.wait_ge(mask1_ready, 16 * (b + 1))
                    settle(sp)
                    sp.dma_start(mask_h[:, r], mask_a1[:, r]).then_inc(maskh_ready[r], 16)

            def stack_parts(c, b, tiles):
                for j in "QK":
                    sp.wait_ge(hi_ready[j], DC * b + c + 1)
                    settle(sp)
                    sp.wait_ge(lo_ready[j], DC * b + c + 1)
                    settle(sp)
                sp.dma_start(bounce[c].rearrange("g d a n -> (g d) a n"), parts[:, c]).then_inc(bounced[c], 16)
                sp.wait_ge(bounced[c], 16 * (b + 1))
                settle(sp)
                if not early(tiles, 1):
                    sp.wait_ge(scores_done, tiles)
                    settle(sp)
                for s in range(4):
                    qa, ka = s // 2, 2 + s % 2
                    for dst, a in ((0, qa), (1, ka)):
                        sp.dma_start(stack[HD * s:HD * s + HD, 4 * c:4 * c + 4, dst, :],
                                     bounce[c, :, :, a, :].rearrange("g d n -> d g n")).then_inc(stacked[c], 16)

            load_adj(1, 0)
            copy_mask1(0)
            load_x(1)
            load_adj(1, 1)
            copy_maskh(0, 2 * NT, 0)
            copy_mask1(1)
            stack_parts(0, 0, 0)
            stack_parts(1, 0, 0)
            with sp.Fori(0, LOOPS) as i:
                q0 = slots_before(i)
                load_x(i + 2)
                load_adj(i + 2, 0)
                load_adj(i + 2, 1)
                stack_parts(0, i + 1, (q0 + 3) * NT)
                copy_maskh(i + 1, (q0 + 7) * NT, 1)
                copy_mask1(i + 2)
                stack_parts(1, i + 1, (q0 + 8) * NT)
            q0 = slots_before(LOOPS)
            stack_parts(0, LOOPS + 1, (q0 + 3) * NT)
            copy_maskh(LOOPS + 1, (q0 + 6) * NT, 1)
            stack_parts(1, LOOPS + 1, (q0 + 7) * NT)
            for t in range(NT):
                sp.wait_ge(last_rows, t + 1)
                sp.dma_start(out_v[NB - 1][:, t], y_f[:, t]).then_inc(last_stored, 16)
            sp.wait_ge(last_stored, 16 * NT)

        @blk.gpsimd
        def _(pool):
            pool.memset(ident[:], 1.0).then_inc(ident_zero, 1)
            pool.memset(minus_half[:], -0.5).then_inc(half_in, 1)
            pool.memset(mean_64[:].bitcast(fp32), 1.0 / 64).then_inc(mean_in, 1)
            pool.wait_ge(ident_zero, 1)
            pool.affine_select(out=ident[:], in_=ident[:], compare_op=ALU.is_equal, fill=0.0, base=0,
                               pattern=[[-1, P]], channel_multiplier=1).then_inc(ident_in, 1)

            def rstd_of(s, c):
                pool.wait_ge(moments_ready[s], c + 1)
                pool.tensor_tensor(rstd[s][:], var_eps[s][:], minus_half[:], ALU.pow).then_inc(rstd_ready[s], 1)

            def gain_and_shift(s, c, y, norm, dst):
                g = gain[:, norm:norm + 1, :].to_broadcast([P, NT, D])
                h = shift[:, norm:norm + 1, :].to_broadcast([P, NT, D])
                pool.tensor_tensor(dst[:], y[:], g, ALU.mult).then_inc(gained[s], 1)
                pool.wait_ge(gained[s], c + 1)
                pool.tensor_tensor(dst[:], dst[:], h, ALU.add).then_inc(ln_done[s], 1)

            def layer_norm_l0(b, l, dst):
                rstd_of("L", 2 * b + l)
                pool.wait_ge(normed["L"], 2 * b + l + 1)
                gain_and_shift("L", 2 * b + l, y_l, l, dst)

            def residual(b):
                pool.wait_ge(ln_done["L"], 2 * b + 2)
                settle(pool)
                pool.tensor_copy(y_f[:], x2[:]).then_inc(xres_ready, 1)

            def finish(b):
                rstd_of("F", b)
                pool.wait_ge(rstd_ready["F"], b + 1)
                settle(pool)
                for t in range(NT):
                    last = pool.tensor_scalar(y_f[:, t], y_f[:, t], minus_mean["F"][:, t:t + 1],
                                              rstd["F"][:, t:t + 1], ALU.add, ALU.mult)
                last.then_inc(normed["F"], 1)
                pool.wait_ge(normed["F"], b + 1)
                gain_and_shift("F", b, y_f, 2, y_f)
                pool.wait_ge(ln_done["F"], b + 1)
                pool.dma_start(out_v[b], y_f[:]).then_inc(out_stored, 16)
                pool.wait_ge(out_stored, 16 * (b + 1))

            pool.wait_ge(weights_in, 16 * N_WEIGHTS_IN)
            pool.tensor_tensor(shift[:, 1], shift[:, 1], bo1, ALU.add).then_inc(bo_added, 1)
            pool.wait_ge(bo_added, 1)
            layer_norm_l0(0, 0, x1)
            layer_norm_l0(0, 1, x2)
            layer_norm_l0(1, 0, x1)
            with pool.Fori(0, LOOPS) as i:
                residual(i)
                layer_norm_l0(i + 1, 1, x2)
                layer_norm_l0(i + 2, 0, x1)
                finish(i)
            residual(NB - 2)
            layer_norm_l0(NB - 1, 1, x2)
            finish(NB - 2)
            residual(NB - 1)
            rstd_of("F", NB - 1)

        @blk.tensor
        def _(pe):
            def bank(pair, half, before):
                name, b, l = before or (None, None, None)
                if name == "S":
                    pe.wait_ge(bias_ready, 1)
                if name == "X":
                    pe.wait_ge(xt_ready, 2 * (2 * b + l) + half + 1)
                if name == "QK":
                    pe.wait_ge(qk_ready, 2 * (2 * b + l) + half + 1)
                if name == "XW":
                    pe.wait_ge(xw_ready, 2 * (2 * b + l) + half + 1)
                if name == "AV":
                    pe.wait_ge(y_ready["L"], 2 * (2 * b + l) + half + 1)
                if name == "X2":
                    pe.wait_ge(xt2_ready, 2 * b + half + 1)
                if name == "QH":
                    pe.wait_ge(lo_ready["QK"[half]], DC * b + l + 1)
                if name == "V":
                    pe.wait_ge(v_ready, 2 * b + half + 1)
                if name == "OG":
                    pe.wait_ge(rb_ready if half else ot_ready, FIRST + 2 * b + l + 1)
                if name == "WO":
                    pe.wait_ge(y_ready["F"], FIRST + 2 * b + half + 1)
                return ps_j[pair][half]

            def scores(q, r, kind, n, b):
                n_tile = NT * q + r
                if not early(n_tile, 2):
                    pe.wait_ge(masked, n_tile - 1)
                if kind == "L":
                    if r == 0:
                        pe.wait_ge(qk_ready, 2 * (2 * b + n) + 2)
                    for n_, (a, c) in enumerate(PART_PAIRS):
                        last = pe.matmul(ps_s[r % 2][:], qt0[:, a, r * P:(r + 1) * P], kt0[:, c],
                                         start=n_ == 0, stop=n_ == 2)
                    last.then_inc(scores_done, 1)
                else:
                    if r == 0 and n % 4 == 0:
                        pe.wait_ge(stacked[n // 4], 16 * 8 * (b + 1))
                    pe.matmul(ps_s[r % 2][:], stack[:, n, 0, r * P:(r + 1) * P], stack[:, n, 1, :],
                              start=True, stop=True).then_inc(scores_done, 1)

            def split_product(dst, lhs, rhs, chunks=DC, more=False):
                terms = [(a, c, e) for e in range(chunks) for a, c in PART_PAIRS]
                for n, (a, c, e) in enumerate(terms):
                    last = pe.matmul(dst, lhs(a, e), rhs(c, e), start=n == 0,
                                     stop=n == len(terms) - 1 and not more)
                return last

            def transposes(q, r, kind, n, b, before_last):
                pe.wait_ge(exps, NT * q + r + 1)
                if before_last is not None and before_last[2] == "L":
                    q_, r_, _, l, b_ = before_last
                    pe.wait_ge(pt_lo_ready, NT * (2 * b_ + l) + r_ + 1)
                if not early(NT * q + r, 2):
                    pe.wait_ge(*(copied(q, r - 2) if r >= 2 else copied(q - 1, r + 2)))
                for t in range(NT):
                    last = pe.transpose(ps_t[r % 2][:, t], probs[:, r, t * P:(t + 1) * P], ident[:])
                last.then_inc(transposed, 1)

            def job(name, pair, b, l, half, before, blk_):
                L = 2 * b + l
                if name == "S":
                    def shift_through(n, w, c0, shift_n):
                        for c in range(DC):
                            last = pe.matmul(ps_j[pair][1][:, n:n + 1], w(c)[:, c0:c0 + P],
                                             shift_c[:, shift_n, c:c + 1], start=c == 0, stop=c == DC - 1)
                        return last

                    bank(pair, 0, before)
                    bank(pair, 1, before)
                    pe.wait_ge(weights0_in, 16 * N_WEIGHTS0_IN)
                    pe.wait_ge(wide_ready, 1)
                    for n, w in enumerate((raw["wc0"][:, DC * D:], raw["wv1"])):
                        for c in range(DC):
                            pe.matmul(ps_j[pair][0][:, n * D:(n + 1) * D], shift_wide[:, n, c],
                                      w[:, c * D:(c + 1) * D], start=c == 0, stop=c == DC - 1)
                    for n, raw_n in enumerate(("wq0", "wk0")):
                        shift_through(n, lambda c: raw[raw_n][:, (DC + c) * F:(DC + c + 1) * F], 0, 0)
                    for n, raw_n in enumerate(("wq1", "wk1")):
                        for g in range(DC):
                            last = shift_through(2 + 2 * n + g, lambda c: raw[raw_n][:, c * D:(c + 1) * D], g * P, 1)
                    last.then_inc(bias_sums, 1)
                if name == "X":
                    if l == 0:
                        pe.wait_ge(x_in, 16 * (b + 1))
                    else:
                        pe.wait_ge(normed["L"], 2 * b + 1)
                    src = y_l if l else x0
                    out_bank = bank(pair, half, before)
                    for t in range(NT):
                        last = pe.transpose(out_bank[:, t * P:(t + 1) * P], src[:, t, half * P:(half + 1) * P], ident[:])
                    last.then_inc(done["X"], 1)
                if name == "X2":
                    if early(b, 1) and half == 0:
                        pe.wait_ge(weights_in, 16 * N_WEIGHTS_IN)
                    pe.wait_ge(normed["L"], 2 * b + 2)
                    out_bank = bank(pair, half, before)
                    for t in range(NT):
                        last = pe.transpose(out_bank[:, t * P:(t + 1) * P], y_l[:, t, half * P:(half + 1) * P], ident[:])
                    last.then_inc(done["X2"], 1)
                if name == "QK":
                    pe.wait_ge(xt_ready, 2 * L + 2)
                    if early(L, 2) and half == 0:
                        pe.wait_ge(weights_ready, L + 1)
                    out_bank = bank(pair, half, before)
                    w = (wq0, wk0)[half]
                    last = split_product(out_bank[:], lambda a, c: w[:, a, l, c], lambda a, c: xt[:, a, c])
                    last.then_inc(done["QK"], 1)
                if name == "AV":
                    r = half
                    pe.wait_ge(pt_lo_ready, NT * L + r + 1)
                    if r == 0:
                        pe.wait_ge(xw_ready, 2 * L + 2)
                    out_bank = bank(pair, r // 2, before if r % 2 == 0 else None)
                    at = (r % 2) * D
                    last = split_product(out_bank[:, at:at + D], lambda a, t: pt_l[:, a, t, r * P:(r + 1) * P],
                                         lambda a, t: xw[:, a, t], NT)
                    last.then_inc(done["AV"], 1)
                if name == "XW":
                    pe.wait_ge(xt_ready, 2 * L + 2)
                    out_bank = bank(pair, half, before)
                    for t in range(2):
                        at = (2 * half + t) * P
                        last = split_product(out_bank[:, t * D:(t + 1) * D], lambda a, c: xt[:, a, c, at:at + P],
                                             lambda a, c: wc0[:, a, l, c], more=l == 1)
                        if l == 1:
                            last = pe.matmul(out_bank[:, t * D:(t + 1) * D], mean_64[:], bx1[:],
                                             start=False, stop=True)
                    last.then_inc(done["XW"], 1)
                if name == "QH":
                    pe.wait_ge(xt2_ready, 2 * b + 2)
                    if early(b, 1) and half == 0:
                        pe.wait_ge(weights_ready, 3)
                    out_bank = bank(pair, half, before)
                    w = (wq1, wk1)[half]
                    last = split_product(out_bank[:], lambda a, c: w[:, a, c, l * P:(l + 1) * P],
                                         lambda a, c: xt2[:, a, c])
                    last.then_inc(done["QK"[half]], 1)
                if name == "V":
                    pe.wait_ge(xt2_ready, 2 * b + 2)
                    out_bank = bank(pair, half, before)
                    for t in range(2):
                        at = (2 * half + t) * P
                        last = split_product(out_bank[:, t * D:(t + 1) * D],
                                             lambda a, c: xt2[:, a, c, at:at + P], lambda a, c: wv1[:, a, c])
                    last.then_inc(done["V"], 1)
                if name == "OG":
                    g, r = l, half
                    if r < 2:
                        for tile in range(2 * r, 2 * r + 2):
                            pe.wait_ge(*copied(blk_.slot_of("H", 4 * g + 3, b), tile))
                        if r == 0:
                            pe.wait_ge(v_ready, 2 * b + 2)
                        out_bank = bank(pair, 0, before if r == 0 else None)
                        for t in range(NT):
                            for h in range(4):
                                col = (4 * g + h) * HD
                                last = pe.matmul(out_bank[h * HD:(h + 1) * HD, 2 * r * P:2 * (r + 1) * P],
                                                 v1[:, t, col:col + HD], pt_h[:, h, t, 2 * r * P:2 * (r + 1) * P],
                                                 start=t == 0, stop=t == NT - 1)
                        last.then_inc(done["O"], 1)
                    else:
                        pe.wait_ge(r_wide_ready, 2 * b + g + 1)
                        out_bank = bank(pair, 1, before)
                        for t in range(NT):
                            last = pe.transpose(out_bank[:, t * P:(t + 1) * P],
                                                r_wide[:, t].rearrange("p h d -> p (h d)"), ident[:])
                        last.then_inc(done["RB"], 1)
                if name == "WO":
                    pe.wait_ge(ot_ready, FIRST + 2 * b + 2)
                    out_bank = bank(pair, half, before)
                    for t in range(2):
                        at = (2 * half + t) * P
                        for g in range(2):
                            last = pe.matmul(out_bank[:, t * D:(t + 1) * D], ot[:, g, at:at + P], wo1[:, g],
                                             start=g == 0, stop=g == 1)
                    last.then_inc(done["WO"], 1)

            def walk(b_):
                for j in b_.pre:
                    job(*j, b_)
                for k in range(b_.n):
                    ahead = b_.tiles_at(k, AHEAD)
                    if k == 0 and not b_.before:
                        for t in ahead:
                            scores(*t)
                        ahead = []
                    transposes(*b_.tile(k), b_.tile(k - 2) if k >= 2 else None)
                    for t in ahead:
                        scores(*t)
                    for j in b_.jobs.get(k, ()):
                        job(*j, b_)

            pe.sem_inc(done["RB"], FIRST)
            pe.wait_ge(ident_in, 1)
            pe.wait_ge(mean_in, 1)
            program(walk, pe.Fori)

        @blk.scalar
        def _(act):
            def exp(q, r, kind, n, b):
                tile = NT * q + r
                act.wait_ge(masked, tile + 1)
                if not early(tile, 4):
                    act.wait_ge(transposed, tile - 3)
                nm, total = (nm_l, sum_l) if kind == "L" else (nm_h, sum_h)
                act.activation(probs[:, r], masked_s[:, r], ACT.Exp, bias=nm[:, n, r:r + 1], scale=-1.0,
                               accum_out=total[:, n, r:r + 1]).then_inc(exps, 1)

            def copy_tile(q, r, kind, n, b):
                act.wait_ge(transposed, NT * q + r + 1)
                dst = (pt_l[:, 0] if kind == "L" else pt_h[:, n % 4])[:, :, r * P:(r + 1) * P]
                act.activation(dst, ps_t[r % 2][:], ACT.Copy).then_inc(copied_act, 1)

            def job(name, pair, b, l, half, before, blk_):
                L = 2 * b + l
                if name == "S":
                    act.wait_ge(weights0_in, 16 * N_WEIGHTS0_IN)
                    for full, part in split_weights[0]:
                        act.activation(part(0), full, ACT.Copy).then_inc(weights_hi, 1)
                    act.wait_ge(biases_in, 16 * N_BIASES_IN)
                if name == "W":
                    act.wait_ge(scaled, l)
                    for full, part in split_weights[l]:
                        act.activation(part(0), full, ACT.Copy).then_inc(weights_hi, 1)
                if pair is None:
                    return
                bank = ps_j[pair][half % 2][:]
                if name == "X":
                    act.wait_ge(done["X"], 2 * L + half + 1)
                    act.activation(xt[:, 0, half], bank, ACT.Copy).then_inc(xt_hi, 1)
                if name == "X2":
                    act.wait_ge(done["X2"], 2 * b + half + 1)
                    act.activation(xt2[:, 0, half], bank, ACT.Copy).then_inc(xt2_hi, 1)
                if name == "QK":
                    act.wait_ge(done["QK"], 2 * L + half + 1)
                    dst, bias = ((qt0, bq0), (kt0, bk0))[half]
                    act.activation(dst[:, 0], bank, ACT.Identity, bias=bias[:, l:l + 1]).then_inc(qk_hi, 1)
                if name == "XW":
                    act.wait_ge(done["XW"], 2 * L + half + 1)
                    act.activation(xw[:, 0, 2 * half:2 * half + 2].rearrange("p t e -> p (t e)"), bank, ACT.Copy)\
                        .then_inc(xw_hi, 1)
                if name == "QH":
                    act.wait_ge(done["QK"[half]], DC * b + l + 1)
                    if not early(b, 1):
                        act.wait_ge(bounced[l], 16 * b)
                    bias = (bq1, bk1)[half]
                    act.activation(parts[:, l, 2 * half], bank, ACT.Identity, bias=bias[:, l:l + 1])\
                        .then_inc(hi_ready["QK"[half]], 1)
                if name == "OG" and half == 2:
                    g = l
                    act.wait_ge(done["RB"], FIRST + 2 * b + g + 1)
                    act.wait_ge(ot_ready, FIRST + 2 * b + g)
                    act.activation(rb[:], ps_j[pair][1][:], ACT.Copy).then_inc(rb_ready, 1)

            def walk(b_):
                for j in b_.pre:
                    job(*j, b_)
                for k in range(b_.n):
                    for t in b_.tiles_at(k, 1):
                        exp(*t)
                    copy_now(b_, k)
                    for j in b_.late_jobs(k):
                        job(*j, b_)

            def copy_now(b_, k):
                t = b_.tile(k)
                if not by_dve(*t[:2]):
                    copy_tile(*t)

            act.sem_inc(rb_ready, FIRST)
            program(walk, act.Fori)

        @blk.vector
        def _(dve):
            def mask(q, r, kind, n, b):
                tile = NT * q + r
                dve.wait_ge(scores_done, tile + 1)
                if not early(tile, 4):
                    dve.wait_ge(exps, tile - 3)
                if kind == "L":
                    if r == 0:
                        dve.wait_ge(*((mask1_ready, 16 * (b + 1)) if n else (mask0_ready, 2 * (b + 1))))
                    m, nm, scale = (mask_a0, mask_a1)[n], nm_l, L0_SCALE
                else:
                    if n == 0:
                        dve.wait_ge(maskh_ready[r], 16 * (b + 1))
                    m, nm, scale = mask_h, nm_h, L1_SCALE
                settle(dve)
                dve.tensor_tensor_reduce(out=masked_s[:, r], in0=ps_s[r % 2][:], in1=m[:, r], scale=-scale,
                                         scalar=BIG, op0=ALU.add, op1=ALU.min,
                                         accum_out=nm[:, n, r:r + 1]).then_inc(masked, 1)

            def copy_tile(q, r, kind, n, b):
                dve.wait_ge(transposed, NT * q + r + 1)
                dst = (pt_l[:, 0] if kind == "L" else pt_h[:, n % 4])[:, :, r * P:(r + 1) * P]
                dve.tensor_copy(dst, ps_t[r % 2][:]).then_inc(copied_dve, 1)

            def low_tile(q, r, kind, n, b):
                dve.wait_ge(transposed, NT * q + r + 1)
                dve.wait_ge(*copied(q, r))
                at = slice(r * P, (r + 1) * P)
                low_part(pt_l[:, 1, :, at], ps_t[r % 2][:], pt_l[:, 0, :, at].bitcast(fp32), pt_lo_ready)

            def statistics(s, c, y, half):
                dve.wait_ge(y_ready[s], (FIRST if s == "F" else 0) + 2 * c + half + 1)
                for t in range(2 * half, 2 * half + 2):
                    last = dve.bn_stats(stats[s][:, t], y[:, t])
                last.then_inc(stats_ready[s], 1)
                if half == 1:
                    dve.wait_ge(stats_ready[s], 2 * c + 2)
                    settle(dve)
                    for t in range(NT):
                        last = dve.bn_aggr(moments[s][:, t], stats[s][:, t])
                    last.then_inc(aggregated[s], 1)
                    dve.wait_ge(aggregated[s], c + 1)
                    dve.tensor_scalar(minus_mean[s][:], moments[s][:, :, 0], -1.0, None, ALU.mult)
                    dve.tensor_scalar(var_eps[s][:], moments[s][:, :, 1], LN_EPS, None, ALU.add)\
                        .then_inc(moments_ready[s], 1)

            def low_part(dst, full, high, ready):
                dve.tensor_tensor(dst, full, high, ALU.subtract).then_inc(ready, 1)

            def low_weights(n):
                for m, (full, part) in enumerate(split_weights[n]):
                    dve.wait_ge(weights_hi, n * len(split_weights[n]) + m + 1)
                    last = dve.tensor_tensor(part(1), full, part(0).bitcast(fp32), ALU.subtract)
                last.then_inc(weights_ready, 1)

            def make_mask(b, h):
                if h == 0 and not early(b, 1):
                    dve.wait_ge(mask1_ready, 16 * b)
                dve.wait_ge(adj_in, 16 * (2 * b + h + 1))
                settle(dve)
                src = adj_spare if early(b, 1) and h == 1 else adj_t[:]
                dve.tensor_scalar(mask_a0[:, 2 * h:2 * h + 2], src, 0.0, MASKED, ALU.is_equal,
                                  ALU.mult).then_inc(mask0_ready, 1)

            def job(name, pair, b, l, half, before, blk_):
                L = 2 * b + l
                if name == "S":
                    dve.wait_ge(weights0_in, 16 * N_WEIGHTS0_IN)
                    dve.tensor_copy(shift_wide, shift_c[:].unsqueeze(3).to_broadcast([P, 2, DC, P]))\
                        .then_inc(wide_ready, 1)
                    low_weights(0)
                    dve.wait_ge(biases_in, 16 * N_BIASES_IN)
                    dve.wait_ge(bias_sums, 1)
                    sums, wide_sums = ps_j[pair][1], ps_j[pair][0]
                    dve.tensor_tensor(bq0[:, 1:2], bq0[:, 1:2], sums[:, 0:1], ALU.add)
                    dve.tensor_tensor(bk0[:, 1:2], bk0[:, 1:2], sums[:, 1:2], ALU.add)
                    dve.tensor_tensor(bq1[:], bq1[:], sums[:, 2:4], ALU.add)
                    dve.tensor_tensor(bk1[:], bk1[:], sums[:, 4:6], ALU.add)
                    dve.tensor_copy(bx1[:], wide_sums[:, 0:D]).then_inc(bx1_hi, 1)
                    dve.wait_ge(bx1_hi, 1)
                    lower = slice(P // 2, P)
                    dve.tensor_tensor(bx1[lower], wide_sums[lower, 0:D], bx1[lower].bitcast(fp32), ALU.subtract)
                    dve.tensor_tensor(bv1[:], bv1[:], wide_sums[:, D:2 * D], ALU.add).then_inc(bias_ready, 1)
                    make_mask(0, 0)
                    make_mask(0, 1)
                if name == "W":
                    names = ((("wq0", F), ("wk0", F), ("wc0", D)), (("wq1", D), ("wk1", D), ("wv1", D)))[l - 1]
                    first = DC if l == 1 else 0
                    for c in range(DC):
                        for raw_n, width in names:
                            w = raw[raw_n][:, (first + c) * width:(first + c + 1) * width]
                            last = dve.tensor_scalar(w, w, gain_c[:, l - 1, c:c + 1], None, ALU.mult)
                    last.then_inc(scaled, 1)
                    low_weights(l)
                if name == "M":
                    make_mask(b, l)
                if name in "SWM":
                    return
                if name == "N":
                    dve.wait_ge(rstd_ready["L"], L + 1)
                    for t in range(NT):
                        last = dve.tensor_scalar(y_l[:, t], y_l[:, t], minus_mean["L"][:, t:t + 1],
                                                 rstd["L"][:, t:t + 1], ALU.add, ALU.mult)
                    last.then_inc(normed["L"], 1)
                    return
                if name == "R":
                    g = l
                    G = 2 * b + g
                    dve.wait_ge(exps, NT * (blk_.slot_of("H", 4 * g + 3, b) + 1))
                    heads = slice(4 * g, 4 * g + 4)
                    dve.scalar_tensor_tensor(sum_f[:], nm_h[:, heads], ALL_MASKED, sum_h[:, heads],
                                             ALU.is_lt, ALU.mult).then_inc(sum_f_ready, 1)
                    dve.wait_ge(sum_f_ready, G + 1)
                    dve.reciprocal(r_h[:], sum_f[:]).then_inc(r_h_ready, 1)
                    dve.wait_ge(r_h_ready, G + 1)
                    dve.wait_ge(done["RB"], FIRST + G)
                    dve.tensor_copy(r_wide.rearrange("p t h d -> p h t d"),
                                    r_h[:].unsqueeze(3).to_broadcast([P, 4, NT, HD]))\
                        .then_inc(r_wide_ready, 1)
                    return
                bank = ps_j[pair][half % 2][:]
                two = bank.rearrange("p (t d) -> p t d", t=2)
                nts = slice(2 * half, 2 * half + 2)
                if name == "X":
                    dve.wait_ge(xt_hi, 2 * L + half + 1)
                    low_part(xt[:, 1, half], bank, xt[:, 0, half].bitcast(fp32), xt_ready)
                if name == "X2":
                    dve.wait_ge(xt2_hi, 2 * b + half + 1)
                    low_part(xt2[:, 1, half], bank, xt2[:, 0, half].bitcast(fp32), xt2_ready)
                if name == "QK":
                    dve.wait_ge(qk_hi, 2 * L + half + 1)
                    dst, bias = ((qt0, bq0), (kt0, bk0))[half]
                    dve.scalar_tensor_tensor(dst[:, 1], bank, bias[:, l:l + 1], dst[:, 0].bitcast(fp32),
                                             ALU.add, ALU.subtract).then_inc(qk_ready, 1)
                if name == "XW":
                    dve.wait_ge(xw_hi, 2 * L + half + 1)
                    low_part(xw[:, 1, nts], two, xw[:, 0, nts].bitcast(fp32), xw_ready)
                if name == "AV" and half % 2 == 1:
                    if half == 1:
                        dve.wait_ge(done["AV"], NT * L + 2)
                        dve.reciprocal(rinv_l[:], sum_l[:, l]).then_inc(rinv_ready, 1)
                        dve.wait_ge(rinv_ready, L + 1)
                        dve.scalar_tensor_tensor(r_l[:], nm_l[:, l], ALL_MASKED, rinv_l[:], ALU.is_lt,
                                                 ALU.mult).then_inc(r_l_ready, 1)
                        dve.wait_ge(r_l_ready, L + 1)
                        if not early(L, 1):
                            dve.wait_ge(ln_done["L"], L)
                        if l == 0:
                            dve.wait_ge(x_in, 16 * (b + 1))
                        else:
                            dve.wait_ge(ln_done["L"], 2 * b + 1)
                    dve.wait_ge(done["AV"], NT * L + half + 1)
                    src = x1 if l else x0
                    for t in range(2):
                        nt = half - 1 + t
                        last = dve.scalar_tensor_tensor(y_l[:, nt], ps_j[pair][half // 2][:, t * D:(t + 1) * D],
                                                        r_l[:, nt:nt + 1], src[:, nt], ALU.mult, ALU.add)
                    last.then_inc(y_ready["L"], 1)
                    statistics("L", L, y_l, half // 2)
                if name == "QH":
                    j = "QK"[half]
                    dve.wait_ge(hi_ready[j], DC * b + l + 1)
                    bias = (bq1, bk1)[half]
                    dve.scalar_tensor_tensor(parts[:, l, 2 * half + 1], bank, bias[:, l:l + 1],
                                             parts[:, l, 2 * half], ALU.add, ALU.subtract)\
                        .then_inc(lo_ready[j], 1)
                if name == "V":
                    dve.wait_ge(done["V"], 2 * b + half + 1)
                    dve.tensor_tensor(v1[:, nts], two, bv1[:].unsqueeze(1).to_broadcast([P, 2, D]), ALU.add)\
                        .then_inc(v_ready, 1)
                if name == "OG" and half == 2:
                    g = l
                    dve.wait_ge(done["O"], 2 * (2 * b + g + 1))
                    dve.wait_ge(rb_ready, FIRST + 2 * b + g + 1)
                    dve.tensor_tensor(ot[:, g], ps_j[pair][0][:], rb[:], ALU.mult).then_inc(ot_ready, 1)
                if name == "WO":
                    dve.wait_ge(done["WO"], 2 * b + half + 1)
                    dve.wait_ge(xres_ready, b + 1)
                    dve.tensor_tensor(y_f[:, nts], two, y_f[:, nts], ALU.add).then_inc(y_ready["F"], 1)
                    statistics("F", b, y_f, half)

            def walk(b_):
                for j in b_.pre:
                    job(*j, b_)
                for k in range(b_.n):
                    for t in b_.tiles_at(k, 2):
                        mask(*t)
                    t = b_.tile(k)
                    if by_dve(*t[:2]):
                        copy_tile(*t)
                    if t[2] == "L":
                        low_tile(*t)
                    for j in b_.late_jobs(k):
                        job(*j, b_)

            dve.sem_inc(y_ready["F"], FIRST)
            dve.sem_inc(ot_ready, FIRST)
            program(walk, dve.Fori)
            dve.wait_ge(weights_in, 16 * N_WEIGHTS_IN)
            dve.wait_ge(moments_ready["F"], NB)
            for t in range(NT):
                dve.scalar_tensor_tensor(y_f[:, t], y_f[:, t], minus_mean["F"][:, t:t + 1], gain[:, 2],
                                         ALU.add, ALU.mult).then_inc(normed["F"], 1)
            dve.wait_ge(rstd_ready["F"], NB)
            for t in range(NT):
                dve.wait_ge(normed["F"], NB - 1 + t + 1)
                dve.scalar_tensor_tensor(y_f[:, t], y_f[:, t], rstd["F"][:, t:t + 1], shift[:, 2],
                                         ALU.mult, ALU.add).then_inc(last_rows, 1)


def kernel(**inputs):
    import numpy as _np
    import concourse.bacc as _bacc
    from concourse import mybir as _mybir
    from concourse.bass_utils import run_bass_kernel_spmd as _run

    nc = _bacc.Bacc("TRN2", target_bir_lowering=False, num_devices=1)
    arrays = {}

    def dram(name, a):
        a = _np.ascontiguousarray(a)
        arrays[name] = a
        return nc.dram_tensor(name, a.shape, _mybir.dt.from_np(a.dtype), kind="ExternalInput").ap()

    def arr(name):
        return _np.asarray(inputs[name])

    x = dram("x_dram", arr("x"))
    adj = dram("adj_dram", arr("adj"))
    l0 = {
        "Wq": dram("l0_wq", arr("L0_gnn_Wq").transpose(0, 2, 1)),
        "Wk": dram("l0_wk", arr("L0_gnn_Wk").transpose(0, 2, 1)),
        "Wc": dram("l0_wc", arr("L0_gnn_Wc").transpose(0, 2, 1)),
        "bq": dram("l0_bq", arr("L0_gnn_bq").T),
        "bk": dram("l0_bk", arr("L0_gnn_bk").T),
        "g": dram("l0_g", arr("L0_gnn_ln_g")),
        "g_c": dram("l0_g_columns", arr("L0_gnn_ln_g").reshape(2 * DC, P).T),
        "b_c": dram("l0_b_columns", arr("L0_gnn_ln_b").reshape(2 * DC, P).T),
        "b": dram("l0_b", arr("L0_gnn_ln_b")),
    }
    l1 = {
        "Wq": dram("l1_wq", arr("L1_gnn_Wq")),
        "Wk": dram("l1_wk", arr("L1_gnn_Wk")),
        "Wv": dram("l1_wv", arr("L1_gnn_Wv")),
        "Wo": dram("l1_wo", arr("L1_gnn_Wo")),
        "bq": dram("l1_bq", arr("L1_gnn_bq").reshape(2, 128).T),
        "bk": dram("l1_bk", arr("L1_gnn_bk").reshape(2, 128).T),
        "bv": dram("l1_bv", arr("L1_gnn_bv")),
        "bo": dram("l1_bo", arr("L1_gnn_bo")),
        "g": dram("l1_g", arr("L1_gnn_gamma")),
        "b": dram("l1_b", arr("L1_gnn_beta")),
    }
    out = nc.dram_tensor("out_dram", arrays["x_dram"].shape, _mybir.dt.float32, kind="ExternalOutput").ap()
    graph_attention(nc, x, adj, l0, l1, out)
    r = _run(nc, [arrays], core_ids=[0])
    return r.results[0]["out_dram"]
```
